# Optimizing a Trainium2 kernel written in Bass

```python
import numpy as np
import jax
import jax.numpy as jnp

def _softmax(x, axis=-1):
    return jax.nn.softmax(x, axis=axis)

def _gelu(x):
    return jax.nn.gelu(x, approximate=True)

def _silu(x):
    return jax.nn.silu(x)

def _sigmoid(x):
    return jax.nn.sigmoid(x)

def _layernorm(x, axis=-1, eps=1e-05):
    m = jnp.mean(x, axis=axis, keepdims=True)
    v = jnp.var(x, axis=axis, keepdims=True)
    return (x - m) / jnp.sqrt(v + eps)

def _scatter_add(tgt, idx, src, axis=0):
    return tgt.at[idx].add(src)

def _segment_sum(src, seg, n):
    return jax.ops.segment_sum(src, seg, n)
kernel_name = 'mk_vit_tower_d1_tok_img768_r4_bdcd62'

def setup_inputs(seed: int=0):
    np.random.seed(seed)
    _w = jnp.asarray

    def _rec_inputs():
        import jax
        import jax.numpy as jnp
        _rk = jax.random.key(seed)
        x = -0.00016672 + 0.999947 * jax.random.normal(jax.random.fold_in(_rk, 1), (16, 96, 96, 3), jnp.float32)
        return x
    x = _rec_inputs()

    def _L0_tok_setup():
        import jax, jax.numpy as jnp
        import numpy as np
        PATCH = 16

        def _extract_patches(images, p):
            B, H, W, C = images.shape
            nh, nw = (H // p, W // p)
            x = images.reshape(B, nh, p, nw, p, C)
            x = x.transpose(0, 1, 3, 2, 4, 5)
            return x.reshape(B, nh * nw, p * p * C)
        key = jax.random.key(seed)
        k1, k2, k3 = jax.random.split(key, 3)
        B, H, Wd, C = (64, 96, 96, 3)
        d_model = 192
        patch_dim = PATCH * PATCH * C
        num_patches = H // PATCH * (Wd // PATCH)
        images = jax.random.normal(k1, (B, H, Wd, C), dtype=jnp.float32)
        W_proj = jax.random.normal(k2, (patch_dim, d_model), dtype=jnp.float32) * (1.0 / np.sqrt(patch_dim))
        b_proj = jnp.zeros((d_model,), dtype=jnp.float32)
        pos_emb = jax.random.normal(k3, (num_patches, d_model), dtype=jnp.float32) * 0.02
        return {'images': images, 'W_proj': W_proj, 'b_proj': b_proj, 'pos_emb': pos_emb}
    _L0_tok_all = _L0_tok_setup()
    _L0_tok_in = {k: v for k, v in _L0_tok_all.items() if k in ('W_proj', 'b_proj', 'pos_emb')}
    del _L0_tok_all

    def _L0_attn_setup():
        import jax, jax.numpy as jnp
        import numpy as np
        NUM_HEADS = 12
        key = jax.random.key(seed)
        k1, k2, k3 = jax.random.split(key, 3)
        B, N, C = (8, 512, 192)
        x = jax.random.normal(k1, (B, N, C), dtype=jnp.float32)
        w_qkv = jax.random.normal(k2, (3 * C, C), dtype=jnp.float32) * C ** (-0.5)
        w_proj = jax.random.normal(k3, (C, C), dtype=jnp.float32) * C ** (-0.5)
        b_proj = jnp.zeros((C,), dtype=jnp.float32)
        return {'x': x, 'w_qkv': w_qkv, 'w_proj': w_proj, 'b_proj': b_proj}
    _L0_attn_all = _L0_attn_setup()
    _L0_attn_in = {k: v for k, v in _L0_attn_all.items() if k in ('w_qkv', 'w_proj', 'b_proj')}
    del _L0_attn_all

    def _L0_ffn_setup():
        import jax, jax.numpy as jnp
        import numpy as np
        EPS_NORM = 1e-05
        RMS_EPS = 1e-05

        def _l2_normalize(v):
            n = jnp.sqrt(jnp.sum(v * v, axis=-1, keepdims=True))
            return v / jnp.maximum(n, EPS_NORM)

        def _rms_norm(x, weight, eps):
            ms = jnp.mean(x * x, axis=-1, keepdims=True)
            return x * jax.lax.rsqrt(ms + eps) * weight
        key = jax.random.key(seed)
        ks = jax.random.split(key, 6)
        B, T, D = (8, 1024, 192)
        S, F = (64, 768)
        x = jax.random.normal(ks[0], (B, T, D), dtype=jnp.float32)
        slots = 0.02 * jax.random.normal(ks[1], (S, D), dtype=jnp.float32)
        scale = jnp.ones((S,), dtype=jnp.float32)
        fc1_weight = 0.02 * jax.random.normal(ks[2], (S, D, F), dtype=jnp.float32)
        fc1_bias = jnp.zeros((S, F), dtype=jnp.float32)
        fc2_weight = 0.02 * jax.random.normal(ks[3], (S, F, D), dtype=jnp.float32)
        fc2_bias = jnp.zeros((S, D), dtype=jnp.float32)
        norm_weight = jnp.ones((D,), dtype=jnp.float32)
        return {'x': x, 'slots': slots, 'scale': scale, 'fc1_weight': fc1_weight, 'fc1_bias': fc1_bias, 'fc2_weight': fc2_weight, 'fc2_bias': fc2_bias, 'norm_weight': norm_weight}
    _L0_ffn_all = _L0_ffn_setup()
    _L0_ffn_in = {k: v for k, v in _L0_ffn_all.items() if k in ('slots', 'scale', 'fc1_weight', 'fc1_bias', 'fc2_weight', 'fc2_bias', 'norm_weight')}
    del _L0_ffn_all
    return {'x': x, 'L0_tok_W_proj': _L0_tok_in['W_proj'], 'L0_tok_b_proj': _L0_tok_in['b_proj'], 'L0_tok_pos_emb': _L0_tok_in['pos_emb'], 'L0_attn_w_qkv': _L0_attn_in['w_qkv'], 'L0_attn_w_proj': _L0_attn_in['w_proj'], 'L0_attn_b_proj': _L0_attn_in['b_proj'], 'L0_ffn_slots': _L0_ffn_in['slots'], 'L0_ffn_scale': _L0_ffn_in['scale'], 'L0_ffn_fc1_weight': _L0_ffn_in['fc1_weight'], 'L0_ffn_fc1_bias': _L0_ffn_in['fc1_bias'], 'L0_ffn_fc2_weight': _L0_ffn_in['fc2_weight'], 'L0_ffn_fc2_bias': _L0_ffn_in['fc2_bias'], 'L0_ffn_norm_weight': _L0_ffn_in['norm_weight']}

def reference(x, L0_tok_W_proj, L0_tok_b_proj, L0_tok_pos_emb, L0_attn_w_qkv, L0_attn_w_proj, L0_attn_b_proj, L0_ffn_slots, L0_ffn_scale, L0_ffn_fc1_weight, L0_ffn_fc1_bias, L0_ffn_fc2_weight, L0_ffn_fc2_bias, L0_ffn_norm_weight):
    import jax
    import jax.numpy as jnp

    def _L0_tok_ref(images, W_proj, b_proj, pos_emb):
        import jax, jax.numpy as jnp
        import numpy as np
        PATCH = 16

        def _extract_patches(images, p):
            B, H, W, C = images.shape
            nh, nw = (H // p, W // p)
            x = images.reshape(B, nh, p, nw, p, C)
            x = x.transpose(0, 1, 3, 2, 4, 5)
            return x.reshape(B, nh * nw, p * p * C)
        patches = _extract_patches(images, PATCH)
        proj = jnp.einsum('bnk,kd->bnd', patches, W_proj) + b_proj
        return proj + pos_emb[None, :, :]

    def _L0_attn_ref(x, w_qkv, w_proj, b_proj):
        import jax, jax.numpy as jnp
        import numpy as np
        NUM_HEADS = 12
        B, N, C = x.shape
        H = NUM_HEADS
        D = C // H
        scale = D ** (-0.5)
        qkv = (x @ w_qkv.T).reshape(B, N, 3, H, D).transpose(2, 0, 3, 1, 4)
        q, k, v = (qkv[0], qkv[1], qkv[2])
        attn = jnp.einsum('bhnd,bhmd->bhnm', q, k) * scale
        attn = jax.nn.softmax(attn, axis=-1)
        out = jnp.einsum('bhnm,bhmd->bhnd', attn, v)
        out = out.transpose(0, 2, 1, 3).reshape(B, N, C)
        return out @ w_proj.T + b_proj

    def _L0_ffn_ref(x, slots, scale, fc1_weight, fc1_bias, fc2_weight, fc2_bias, norm_weight):
        import jax, jax.numpy as jnp
        import numpy as np
        EPS_NORM = 1e-05
        RMS_EPS = 1e-05

        def _l2_normalize(v):
            n = jnp.sqrt(jnp.sum(v * v, axis=-1, keepdims=True))
            return v / jnp.maximum(n, EPS_NORM)

        def _rms_norm(x, weight, eps):
            ms = jnp.mean(x * x, axis=-1, keepdims=True)
            return x * jax.lax.rsqrt(ms + eps) * weight
        xn = _rms_norm(x, norm_weight, RMS_EPS)
        tok = _l2_normalize(xn)
        sl = _l2_normalize(slots) * scale[:, None]
        logits = jnp.einsum('sd,btd->bst', sl, tok)
        dispatch_w = jax.nn.softmax(logits, axis=-1)
        combine_w = jax.nn.softmax(logits, axis=-2)
        y = jnp.einsum('btd,bst->bsd', xn, dispatch_w)
        y = jnp.einsum('sio,bsi->bso', fc1_weight, y) + fc1_bias
        y = jax.nn.gelu(y, approximate=False)
        y = jnp.einsum('sio,bsi->bso', fc2_weight, y) + fc2_bias
        out = jnp.einsum('bsd,bst->btd', y, combine_w)
        return out
    h = _L0_tok_ref(x, L0_tok_W_proj, L0_tok_b_proj, L0_tok_pos_emb)
    h = h + _L0_attn_ref(_layernorm(h, axis=-1), L0_attn_w_qkv, L0_attn_w_proj, L0_attn_b_proj)
    h = h + _L0_ffn_ref(_layernorm(h, axis=-1), L0_ffn_slots, L0_ffn_scale, L0_ffn_fc1_weight, L0_ffn_fc1_bias, L0_ffn_fc2_weight, L0_ffn_fc2_bias, L0_ffn_norm_weight)
    return h

_drawn_inputs = setup_inputs


def setup_inputs(seed=0):
    import zlib

    import numpy as np

    out = dict(_drawn_inputs(seed))
    spreads = {'L0_tok_b_proj': (0.0, 0.1),
     'L0_attn_b_proj': (0.0, 0.1),
     'L0_ffn_scale': (1.0, 0.6),
     'L0_ffn_fc1_bias': (0.0, 0.8),
     'L0_ffn_fc2_bias': (0.0, 0.745),
     'L0_ffn_norm_weight': (1.0, 0.6)}
    factors = {'L0_ffn_slots': 8.0,
     'L0_ffn_fc1_weight': 8.0,
     'L0_ffn_fc2_weight': 8.0,
     'L0_tok_pos_emb': 2.76}
    for name, (base, spread) in spreads.items():
        noise = np.random.default_rng([zlib.crc32(name.encode()), seed]).standard_normal(out[name].shape)
        drawn = base * np.exp(spread * noise) if base else spread * noise
        out[name] = jnp.asarray(drawn.astype(out[name].dtype))
    for name, factor in factors.items():
        out[name] = (out[name] * factor).astype(out[name].dtype)
    return out
```

```python
from contextlib import ExitStack

import concourse.bass as bass
from concourse import mybir

F32 = mybir.dt.float32
ALU = mybir.AluOpType
ACT = mybir.ActivationFunctionType
AX = mybir.AxisListType


def vit_tower_kernel(nc, x, tok_w, tok_b, tok_pos, w_qkv, w_proj, attn_b, slots, slot_scale,
                     fc1_w, fc1_b, fc2_w, fc2_b, norm_w, out):
    B, IMG, _, CH = x.shape
    KP, D = tok_w.shape
    N = tok_pos.shape[0]
    GRID = 6
    PATCH = IMG // GRID
    NT = B * N
    HEADS, DH = 12, 16
    S, _, FF = fc1_w.shape
    EPS = 1e-5
    TPI = 3
    TR = TPI * N
    TT = -(-B // TPI)
    HALF = NT // 2
    C2 = D // 2
    OG = 2
    HG = HEADS // OG
    G3 = HEADS // 3
    VW = 3 * DH + 3
    PAIRS = B // 2
    R2 = 64 + N
    QW = HG * N
    SCALE = DH ** -0.5
    GS = 8
    GROUPS = S // GS
    UNITS = 6
    RING = 2 * UNITS
    UF = GS * D * FF // 3 // 128
    FC = FF // 128
    KC = KP // 128
    XR = IMG * CH

    def rows(t):
        return min(TR, NT - TR * t)

    with ExitStack() as ctx:
        def sb(name, shape):
            return ctx.enter_context(nc.sbuf_tensor(name, shape, F32))

        def sem(name):
            return ctx.enter_context(nc.semaphore(name))

        ring = sb("ring", [128, RING, UF])
        EARLY = RING - 6
        early = ring[:, EARLY:RING, :].rearrange("p s n -> p (s n)")
        at = [0]

        def carve(base, *shape):
            n = 1
            for d in shape:
                n *= d
            v = base[:, at[0]:at[0] + n]
            at[0] += n
            if len(shape) == 2:
                v = v.rearrange("p (a b) -> p a b", a=shape[0])
            elif len(shape) == 3:
                v = v.rearrange("p (a b c) -> p a b c", a=shape[0], b=shape[1])
            elif len(shape) == 4:
                v = v.rearrange("p (a b c d) -> p a b c d", a=shape[0], b=shape[1], c=shape[2])
            return v

        x_rows = carve(early, 2, 8 * XR)
        x_patch = carve(early, 2, GRID, KP // 2)
        patchesT = carve(early, KC, NT)
        embed_w = carve(early, KC, D)
        qkv_raw = carve(early, 6, D)
        proj_raw = carve(early, 2, D)
        b1_raw = carve(early, FF)
        assert at[0] <= 6 * UF

        ident = sb("ident", [128, 128])
        h = sb("h", [128, TT, D])
        xn = sb("xn", [128, TT, D])
        xT = sb("xT", [128, 2, NT])
        qkvT = sb("qkvT", [128, 2, 3 * D])
        projT = sb("projT", [128, 2, D])
        pos_b = sb("pos_b", [128, D])
        attn_b_row = sb("attn_b_row", [128, D])
        norm_row = sb("norm_row", [128, D])
        slot_rows = sb("slot_rows", [128, D])
        slotT = sb("slotT", [128, 2, S])
        b1T = sb("b1T", [128, FC, S])
        b2_rows = sb("b2_rows", [128, D])
        head_mask = sb("head_mask", [128, HG])
        image_mask = sb("image_mask", [128, TPI])
        value_mask = sb("value_mask", [128, G3, 3 * DH])
        batch_mask = sb("batch_mask", [128, B])
        stats = sb("stats", [128, TT, 6])
        mv = sb("mv", [128, TT, 2])
        neg_half = sb("neg_half", [128, TT])
        rstd = sb("rstd", [128, TT])
        pv_tmp = sb("pv_tmp", [128, 4, TT])
        ln_scale = sb("ln_scale", [128, TT])
        ssq = sb("ssq", [128, TT])
        rnorm = sb("rnorm", [128, TT])
        slot_sc = sb("slot_sc", [128, 4])
        mx = sb("mx", [128, 2, HEADS])
        rcp = sb("rcp", [128, 2, HEADS])
        soft = sb("soft", [128, 4, B])
        soft_space = sb("soft_space", [128, 2 * NT])
        logits, disp = soft_space[:, 0:NT], soft_space[:, NT:2 * NT]
        x_copies = soft_space[:, 0:2 * 2 * 2 * TR].rearrange("p (i c a n) -> p i c a n", i=2, c=2, a=2)
        pos_raw = disp[:, D:2 * D]

        region_k = sb("region_k", [128, 4032])
        at[0] = 0
        qT = carve(region_k, OG, NT)
        kT = carve(region_k, OG, NT)
        k_diag = carve(region_k, 2, OG, 2 * QW)
        at[0] = 0
        y_diag = carve(region_k, 3, S // 2, 32)
        y2 = carve(region_k, 2, D)
        sel = carve(region_k, 2, 128)
        region_p = sb("region_p", [128, 3200])
        at[0] = 0
        probs = carve(region_p, 2, OG * QW)
        probsT = carve(region_p, 2, G3, R2)
        o_rows = carve(region_p, 2, D)
        oT = carve(region_p, 2, NT)
        at[0] = 0
        gact = carve(region_p, FC, GS, 32)
        hid = carve(region_p, FC, 128)
        pre = carve(region_p, FC, 128)
        v_diag = sb("v_diag", [128, 2, 2, G3 * VW])
        qkv_flat = qkvT[:, :, :].rearrange("p a b -> p (a b)")
        tok = qkv_flat[:, 0:TT * D].rearrange("p (t d) -> p t d", t=TT)
        comb = qkv_flat[:, 0:TT * S].rearrange("p (t s) -> p t s", t=TT)
        y_group = qkv_flat[:, TT * S:TT * S + 768].rearrange("p (g j n) -> p g j n", g=2, j=3)
        combT = v_diag[:, :, :, :].rearrange("p a b c -> p (a b c)")[:, 0:NT]
        xT_flat = xT[:, :, :].rearrange("p a b -> p (a b)")
        disp_diag = xT_flat.rearrange("p (t i s) -> p t i s", t=TT, i=TPI)
        mix = xT

        ps = ctx.enter_context(nc.psum_tensor("ps", [128, 8, 512], F32))

        wqkv_in, wproj_in, wp_in = sem("wqkv_in"), sem("wproj_in"), sem("wp_in")
        x_in = [sem("x_in0"), sem("x_in1")]
        pos_in, ab_in, nw_in = sem("pos_in"), sem("ab_in"), sem("nw_in")
        slots_in, b1_in, b2_in = sem("slots_in"), sem("b1_in"), sem("b2_in")
        unit_in = [sem(f"unit_in{i}") for i in range(RING)]
        units_used = sem("units_used")
        out_written = sem("out_written")
        ident_ready, masks_ready, zeros_ready = sem("ident_ready"), sem("masks_ready"), sem("zeros_ready")
        w_turned, w_kept_a, w_kept_d = sem("w_turned"), sem("w_kept_a"), sem("w_kept_d")
        regrouped_a, regrouped_d = sem("regrouped_a"), sem("regrouped_d")
        x_turned, x_kept_a, x_kept_d = sem("x_turned"), sem("x_kept_a"), sem("x_kept_d")
        embedded, h_ready, moments = sem("embedded"), sem("h_ready"), sem("moments")
        rstd_ready, xn_ready, bias_added = sem("rstd_ready"), sem("xn_ready"), sem("bias_added")
        slots_sq, slots_scaled, slots_ready = sem("slots_sq"), sem("slots_scaled"), sem("slots_ready")
        misc_turned, misc_kept = sem("misc_turned"), sem("misc_kept")
        xn_turned, xT_ready = sem("xn_turned"), sem("xT_ready")
        qk_done, q_ready, k_ready, kdiag_ready = sem("qk_done"), sem("q_ready"), sem("k_ready"), sem("kdiag_ready")
        copies_ready = sem("copies_ready")
        junk_set = sem("junk_set")
        scores_ready, shifted, exp_ready = sem("scores_ready"), sem("shifted"), sem("exp_ready")
        probs_turned, probsT_ready = sem("probs_turned"), sem("probsT_ready")
        v_done, vdiag_ready, pv_done = sem("v_done"), sem("vdiag_ready"), sem("pv_done")
        o_ready, o_turned, oT_ready = sem("o_ready"), sem("o_turned"), sem("oT_ready")
        attn_done, h2_ready, moments2 = sem("attn_done"), sem("h2_ready"), sem("moments2")
        scale2_ready, xn2_ready, sq_ready, rnorm_ready = sem("scale2_ready"), sem("xn2_ready"), sem("sq_ready"), sem("rnorm_ready")
        tok_ready, tok_turned, tokT_ready = sem("tok_ready"), sem("tok_turned"), sem("tokT_ready")
        logits_done, logits_ready, soft_banks = sem("logits_done"), sem("logits_ready"), sem("soft_banks")
        logits_turned = sem("logits_turned")
        d_shifted, d_exp, disp_ready, disp_turned, ddiag_ready = (
            sem("d_shifted"), sem("d_exp"), sem("disp_ready"), sem("disp_turned"), sem("ddiag_ready"))
        c_shifted, c_exp, comb_ready, comb_turned, combT_ready = (
            sem("c_shifted"), sem("c_exp"), sem("comb_ready"), sem("comb_turned"), sem("combT_ready"))
        y_done, y_kept_d, y_kept_a = sem("y_done"), sem("y_kept_d"), sem("y_kept_a")
        ydiag_zero, gact_zero = sem("ydiag_zero"), sem("gact_zero")
        bias2_done = sem("bias2_done")
        group_in, mix_done, mix_ready = sem("group_in"), sem("mix_done"), sem("mix_ready")
        hid_ready, hid_turned = sem("hid_ready"), sem("hid_turned")
        pre_ready, gact_ready = sem("pre_ready"), sem("gact_ready")
        y2_ready, combined, final_ready = sem("y2_ready"), sem("combined"), sem("final_ready")
        dve_step, pool_step = sem("dve_step"), sem("pool_step")

        x_view = x.rearrange("b (n p) w c -> (b n) (p w c)", n=GRID)
        fc1_view = fc1_w.rearrange("s d o -> (s d) o").rearrange("(q p j) o -> j p q o", p=128, j=3)
        fc2_view = fc2_w.rearrange("s (p c) d -> p s c d", p=128)
        out_view = out.rearrange("b n d -> (b n) d")

        def attn_tiles(i):
            found = [t for t in range(TT) if min(TPI * t + TPI - 1, B - 1) // 2 == i - 3]
            return [(t, 6 + (i - 3 + n) % 2) for n, t in enumerate(found)]

        def y_columns(row, t, n):
            return ps[row:row + 64, t % 2, 0:3 * 96].rearrange("p (j b q) -> p j q b", j=3, b=TPI)[:, :, :, 0:n]

        def pixels(ph, a, b):
            src = x_rows[0:C2, ph, :].rearrange("p (r w e) -> p w r e", r=8, w=GRID)[:, a:b]
            dst = x_patch[0:C2, ph, a:b, :].rearrange("p w (r e) -> p w r e", r=8)
            return dst, src

        def earlier(eng, signal, count):
            if not (isinstance(count, int) and count == 0):
                eng.wait_ge(signal, count)

        block = ctx.enter_context(nc.Block())

        @block.sync
        def _(sp):
            sp.dma_start(qkv_raw[0:C2], w_qkv.rearrange("(t p) c -> p t c", p=C2)).then_inc(wqkv_in, 16)
            for ph in range(2):
                sp.dma_start(x_rows[0:C2, ph, :],
                             x_view[:, ph * 8 * XR:(ph + 1) * 8 * XR]).then_inc(x_in[ph], 16)
            sp.dma_start(embed_w[:, :, :], tok_w.rearrange("(c p) d -> p c d", p=128)).then_inc(wp_in, 16)
            sp.dma_start(proj_raw[0:C2], w_proj.rearrange("(t p) c -> p t c", p=C2)).then_inc(wproj_in, 16)

            def load_unit(g, slot):
                u = slot % UNITS
                if u < 3:
                    dst = ring[:, slot, :].rearrange("p (q o) -> p q o", q=GS // 2)
                    src = fc1_view[u][:, bass.ds(g * (GS // 2), GS // 2), :]
                else:
                    dst = ring[:, slot, :].rearrange("p (s n) -> p s n", s=GS)
                    src = fc2_view[:, bass.ds(g * GS, GS), 2 * (u - 3):2 * (u - 3) + 2, :].rearrange(
                        "p s c d -> p s (c d)")
                sp.dma_start(dst, src).then_inc(unit_in[slot], 16)

            for slot in range(RING):
                if slot == EARLY:
                    sp.wait_ge(embedded, TT)
                    sp.wait_ge(misc_turned, 2)
                load_unit(slot // UNITS, slot)
            with sp.Fori(1, GROUPS // 2) as it:
                for slot in range(RING):
                    sp.wait_ge(units_used, it * RING + (slot + 1 - RING))
                    load_unit(it * 2 + slot // UNITS, slot)
            for tt in range(3):
                sp.wait_ge(final_ready, (1, 2, 4)[tt])
                if tt < 2:
                    sp.dma_start(out_view[2 * tt * TR:2 * (tt + 1) * TR, :].rearrange("(t p) d -> p t d", p=TR),
                                 h[0:TR, 2 * tt:2 * tt + 2, :]).then_inc(out_written, 16)
                else:
                    for t in (TT - 2, TT - 1):
                        sp.dma_start(out_view[t * TR:t * TR + rows(t), :],
                                     h[0:rows(t), t, :]).then_inc(out_written, 16)
            sp.wait_ge(out_written, 64)

        @block.gpsimd
        def _(pool):
            steps = [0]

            def step(ins):
                steps[0] += 1
                ins.then_inc(pool_step, 1)
                pool.wait_ge(pool_step, steps[0])

            step(pool.memset(ident[:, :], 0.0))
            step(pool.affine_select(out=ident[:, :], in_=ident[:, :], compare_op=ALU.not_equal, fill=1.0, base=0,
                                    pattern=[[-1, 128]], channel_multiplier=1))
            pool.memset(neg_half[:, :], -0.5).then_inc(ident_ready, 1)
            pool.wait_ge(ident_ready, 1)
            for n, (place, value) in enumerate(((mv[:, :, :], 1.0), (ssq[:, :], 1.0), (qT[96:128, :, :], 0.0),
                                                (k_diag[96:128, :, :, :], 0.0))):
                pool.memset(place, value).then_inc(zeros_ready, 1)
                pool.wait_ge(zeros_ready, n + 1)

            def band(mask, pattern, width):
                step(pool.memset(mask, 1.0))
                step(pool.affine_select(out=mask, in_=mask, compare_op=ALU.is_ge, fill=0.0, base=0,
                                        pattern=[[-w, n] for w, n in pattern], channel_multiplier=1))
                step(pool.affine_select(out=mask, in_=mask, compare_op=ALU.is_ge, fill=0.0, base=width - 1,
                                        pattern=pattern, channel_multiplier=-1))

            band(head_mask[:, :], [[DH, HG]], DH)
            band(image_mask[:, :], [[N, TPI]], N)
            band(value_mask[:, :, :].rearrange("p g (j d) -> p g j d", j=3), [[0, G3], [N, 3], [0, DH]], N)
            v_blocks = v_diag[:, :, :, :].rearrange("p a b (g w) -> p (a b g) w", w=VW)
            pool.tensor_copy(v_blocks[0:TR, :, 3 * DH:VW],
                             image_mask[0:TR, :].unsqueeze(1).to_broadcast([TR, 16, 3])).then_inc(masks_ready, 1)

            for n in range(2):
                a, b = 3 * n, 3 * n + 3
                pool.wait_ge(moments, b)
                if n == 0:
                    pool.wait_ge(masks_ready, 1)
                step(pool.tensor_scalar(pv_tmp[:, 0, a:b], mv[:, a:b, 1], EPS, None, ALU.add))
                pool.tensor_tensor(rstd[:, a:b], pv_tmp[:, 0, a:b], neg_half[:, a:b], ALU.pow).then_inc(rstd_ready, 1)
            pool.wait_ge(slots_sq, 1)
            step(pool.tensor_scalar(slot_sc[0:S, 2:3], slot_sc[0:S, 0:1], EPS * EPS, None, ALU.max))
            step(pool.tensor_tensor(slot_sc[0:S, 3:4], slot_sc[0:S, 2:3], neg_half[0:S, 0:1], ALU.pow))
            pool.wait_ge(slots_in, 32)
            pool.tensor_tensor(slot_sc[0:S, 2:3], slot_sc[0:S, 3:4], slot_sc[0:S, 1:2],
                               ALU.mult).then_inc(slots_scaled, 1)

            def k_blocks(i):
                for og in range(OG):
                    pool.tensor_tensor(
                        k_diag[0:C2, i % 2, og, :].rearrange("p (a h m) -> p a h m", a=2, h=HG),
                        kT[0:C2, og, 2 * N * i:2 * N * (i + 1)].rearrange("p (a m) -> p a m", a=2)
                        .unsqueeze(2).to_broadcast([C2, 2, HG, N]),
                        head_mask[0:C2, :].unsqueeze(1).unsqueeze(3).to_broadcast([C2, 2, HG, N]),
                        ALU.mult).then_inc(kdiag_ready, 1)

            def copy_tokens(i):
                if i >= 2:
                    pool.wait_ge(v_done, i - 1)
                for c in range(2):
                    pool.tensor_copy(x_copies[0:C2, i % 2, c, :, :].rearrange("p a (j n) -> p a j n", j=3),
                                     xT[0:C2, c, 2 * N * i:2 * N * (i + 1)].rearrange("p (a n) -> p a n", a=2)
                                     .unsqueeze(2).to_broadcast([C2, 2, 3, N])).then_inc(copies_ready, 1)

            def ln_bias(i):
                if i == 0:
                    pool.wait_ge(ab_in, 16)
                pool.wait_ge(xn_ready, i + 1)
                pool.tensor_tensor(h[0:rows(i), i, :], h[0:rows(i), i, :], attn_b_row[0:rows(i), :],
                                   ALU.add).then_inc(bias_added, 1)

            for i in range(PAIRS):
                pool.wait_ge(k_ready, 2 if i < 4 else 4)
                if i >= 2:
                    pool.wait_ge(scores_ready, i - 1)
                k_blocks(i)
                copy_tokens(i)
                if i < TT:
                    ln_bias(i)

            for a, b in ((0, 4), (4, TT)):
                pool.wait_ge(moments2, b)
                v, t0, t1, t2, t3 = mv[:, a:b, 1], *(pv_tmp[:, n, a:b] for n in range(4))
                step(pool.tensor_scalar(t0, v, EPS, None, ALU.add))
                step(pool.tensor_tensor(t1, t0, neg_half[:, a:b], ALU.pow))
                step(pool.tensor_tensor(t2, t1, t1, ALU.mult))
                step(pool.tensor_tensor(t3, t2, v, ALU.mult))
                step(pool.tensor_scalar(t0, t3, EPS, None, ALU.add))
                step(pool.tensor_tensor(t2, t0, neg_half[:, a:b], ALU.pow))
                pool.tensor_tensor(ln_scale[:, a:b], t1, t2, ALU.mult).then_inc(scale2_ready, 1)
                pool.wait_ge(sq_ready, b)
                step(pool.tensor_scalar(t0, ssq[:, a:b], EPS * EPS, None, ALU.max))
                pool.tensor_tensor(rnorm[:, a:b], t0, neg_half[:, a:b], ALU.pow).then_inc(rnorm_ready, 1)
            pool.wait_ge(scores_ready, PAIRS)
            pool.memset(y_diag[:, :, :, :], 0.0).then_inc(ydiag_zero, 1)
            pool.wait_ge(attn_done, TT)
            pool.memset(gact[:, :, :, :], 0.0).then_inc(gact_zero, 1)

            pool.wait_ge(y_kept_d, TT)
            pool.wait_ge(y_kept_a, TT)
            pool.wait_ge(combT_ready, 2)

            def bring_group(g, gg):
                pool.tensor_copy(y_group[:, gg, :, :].rearrange("p j (q n) -> p j q n", q=4),
                                 y_diag[:, :, bass.ds(g * 4, 4), :]).then_inc(group_in, 1)
                pool.tensor_copy(sel[0:S, gg, :].rearrange("p (s b) -> p s b", s=GS),
                                 ident[0:S, bass.ds(g * GS, GS)].unsqueeze(2).to_broadcast([S, GS, B])
                                 ).then_inc(group_in, 1)

            for g in range(2):
                bring_group(g, g)
            with pool.Fori(1, GROUPS // 2) as it:
                for gg in range(2):
                    g = it * 2 + gg
                    pool.wait_ge(units_used, g * UNITS + (3 - 2 * UNITS))
                    bring_group(g, gg)

        @block.scalar
        def _(act):
            pos_view = tok_pos
            for j in range(TPI):
                act.dma_start(pos_raw[j * N:(j + 1) * N, :], pos_view).then_inc(pos_in, 16)
            act.dma_start(pos_b[0:TR, :], tok_b.partition_broadcast(TR)).then_inc(pos_in, 16)
            act.dma_start(slot_rows[0:S, :], slots).then_inc(slots_in, 16)
            act.dma_start(slot_sc[0:S, 1:2], slot_scale.rearrange("(s a) -> s a", a=1)).then_inc(slots_in, 16)
            act.dma_start(b1_raw[0:S, :], fc1_b).then_inc(b1_in, 16)
            act.dma_start(attn_b_row[0:TR, :], attn_b.partition_broadcast(TR)).then_inc(ab_in, 16)
            act.dma_start(norm_row[0:TR, :], norm_w.partition_broadcast(TR)).then_inc(nw_in, 16)
            act.dma_start(b2_rows[0:S, :], fc2_b).then_inc(b2_in, 16)

            for t in range(0, 8, 2):
                act.wait_ge(w_turned, t + 1)
                dst = qkvT[0:C2, :, t * C2:(t + 1) * C2] if t < 6 else projT[0:C2, :, (t - 6) * C2:(t - 5) * C2]
                act.copy(dst, ps[0:C2, 4 + t % 4, 0:2 * C2].rearrange("p (c n) -> p c n", c=2)).then_inc(w_kept_a, 1)
            for n in range(0, 12, 2):
                if n % 6 == 0:
                    act.wait_ge(x_in[n // 6], 16)
                    act.copy(*pixels(n // 6, 4, 6)).then_inc(regrouped_a, 1)
                act.wait_ge(x_turned, n + 1)
                ph, nw = n // 6, n % 6
                act.copy(patchesT[:, ph * 3:ph * 3 + 3, nw::GRID],
                         ps[:, n % 4, 0:288].rearrange("p (r n) -> p r n", r=3)).then_inc(x_kept_a, 1)
            act.wait_ge(slots_in, 32)
            act.activation(disp[0:S, 0:D], slot_rows[0:S, :], ACT.Square,
                           accum_out=slot_sc[0:S, 0:1]).then_inc(slots_sq, 1)

            def keep_xT(t):
                act.wait_ge(xn_turned, t + 1)
                act.copy(xT[0:C2, :, t * TR:t * TR + rows(t)],
                         ps[0:C2, t % 2, 0:2 * rows(t)].rearrange("p (c n) -> p c n", c=2)).then_inc(xT_ready, 1)

            def keep_q(half):
                for g in range(2):
                    act.wait_ge(qk_done, half * 4 + g + 1)
                    act.mul(qT[0:C2, g, half * HALF:(half + 1) * HALF],
                            ps[0:C2, 2 + g, 0:HALF], SCALE).then_inc(q_ready, 1)

            for t in range(3):
                keep_xT(t)
            keep_q(0)
            for t in range(3, TT):
                keep_xT(t)
            keep_q(1)
            act.wait_ge(misc_turned, 1)
            act.copy(b1T[:, :, :], ps[:, 6, 0:FC * S].rearrange("p (c s) -> p c s", c=FC)).then_inc(misc_kept, 1)
            act.wait_ge(misc_turned, 2)
            act.copy(slotT[0:C2, :, :], ps[0:C2, 7, 0:2 * S].rearrange("p (c s) -> p c s", c=2)).then_inc(misc_kept, 1)

            for i in range(PAIRS + 2):
                if i < PAIRS:
                    act.wait_ge(shifted, i + 1)
                    act.activation(probs[0:R2, i % 2, :], probs[0:R2, i % 2, :], ACT.Exp).then_inc(exp_ready, 1)
                if 1 <= i <= PAIRS:
                    act.wait_ge(probs_turned, i)
                    if i >= 3:
                        act.wait_ge(pv_done, i - 2)
                    act.copy(probsT[0:TR, (i - 1) % 2, :, :],
                             ps[0:TR, (i - 1) % 2, 0:G3 * R2].rearrange("p (g n) -> p g n", g=G3)
                             ).then_inc(probsT_ready, 1)
                if i >= 2:
                    p = i - 2
                    act.wait_ge(o_turned, p + 1)
                    src = ps[0:C2, 6 + p % 2, 256:256 + 2 * R2].rearrange("p (c n) -> p c n", c=2)
                    for a in range(2):
                        cp = act.copy(oT[0:C2, :, (2 * p + a) * N:(2 * p + a + 1) * N], src[:, :, 64 * a:64 * a + N])
                        cp.then_inc(oT_ready, 1)

            for t in range(TT):
                act.wait_ge(xn2_ready, t + 1)
                act.activation(soft_space[0:rows(t), t * D:(t + 1) * D], xn[0:rows(t), t, :], ACT.Square,
                               accum_out=ssq[0:rows(t), t:t + 1]).then_inc(sq_ready, 1)
            for t in range(TT):
                act.wait_ge(tok_turned, t + 1)
                act.copy(xT[0:C2, :, t * TR:t * TR + rows(t)],
                         ps[0:C2, 2 + t % 2, 0:2 * rows(t)].rearrange("p (c n) -> p c n", c=2)).then_inc(tokT_ready, 1)
            for half in range(2):
                act.wait_ge(logits_done, half + 1)
                act.copy(logits[0:S, half * HALF:(half + 1) * HALF], ps[0:S, 4 + half, 0:HALF]).then_inc(logits_ready, 1)
            act.wait_ge(d_shifted, 1)
            act.activation(disp[0:S, :], disp[0:S, :], ACT.Exp).then_inc(d_exp, 1)
            act.wait_ge(c_shifted, 1)
            act.activation(comb[0:TR, :, :], comb[0:TR, :, :], ACT.Exp).then_inc(c_exp, 1)

            for t in range(TT):
                n = min(TPI, B - TPI * t)
                act.wait_ge(y_done, t + 1)
                if t == 0:
                    act.wait_ge(ydiag_zero, 1)
                act.copy(y_diag[64:128, :, :, B + TPI * t:B + TPI * t + n],
                         y_columns(64, t, n)
                         ).then_inc(y_kept_a, 1)
            act.wait_ge(comb_turned, 1)
            act.copy(combT[0:S, 0:4 * TR], ps[0:S, 6, 0:4 * TR]).then_inc(combT_ready, 1)
            act.wait_ge(comb_turned, 2)
            act.copy(combT[0:S, 4 * TR:NT], ps[0:S, 7, 0:NT - 4 * TR]).then_inc(combT_ready, 1)

            act.wait_ge(gact_zero, 1)
            def mlp_group(g, gg, it):
                act.wait_ge(units_used, g * UNITS + 3)
                earlier(act, hid_turned, g)
                for half in range(2):
                    act.copy(hid[:, :, half * 64:(half + 1) * 64].rearrange("p c n -> p n c"),
                             ps[:, half, 0:FF // 2].rearrange("p (n c) -> p n c", c=FC)).then_inc(hid_ready, 1)
                act.wait_ge(pre_ready, g * 2 + 2)
                earlier(act, units_used, g * UNITS)
                gflat = gact[:, :, :, :].rearrange("p c s n -> p (c s n)").rearrange("p (k n) -> p k n", n=64)
                src = pre[:, :, :].rearrange("p c (q l b) -> p (c q) l b", l=2, b=B)
                for l in range(2):
                    act.activation(gflat[:, :, 48 * l:48 * l + B], src[:, :, l, :], ACT.Gelu).then_inc(gact_ready, 1)
                act.wait_ge(units_used, g * UNITS + 6)
                earlier(act, combined, g * 3)
                act.copy(y2[:, gg, :], ps[:, 4, 0:D]).then_inc(y2_ready, 1)

            for gg in range(2):
                mlp_group(gg, gg, 0)
            with act.Fori(1, GROUPS // 2) as it:
                for gg in range(2):
                    mlp_group(it * 2 + gg, gg, it)

        @block.vector
        def _(dve):
            steps = [0]

            def step(ins):
                steps[0] += 1
                ins.then_inc(dve_step, 1)
                dve.wait_ge(dve_step, steps[0])

            dve.wait_ge(pos_in, 64)
            step(dve.tensor_tensor(pos_b[0:TR, :], pos_b[0:TR, :], pos_raw[0:TR, :], ALU.add))
            for t in range(1, 8, 2):
                dve.wait_ge(w_turned, t + 1)
                dst = qkvT[0:C2, :, t * C2:(t + 1) * C2] if t < 6 else projT[0:C2, :, (t - 6) * C2:(t - 5) * C2]
                dve.tensor_copy(dst, ps[0:C2, 4 + t % 4, 0:2 * C2].rearrange("p (c n) -> p c n", c=2)
                                ).then_inc(w_kept_d, 1)
            for n in range(1, 12, 2):
                if n % 6 == 1:
                    for a in (0, 2):
                        dve.wait_ge(x_in[n // 6], 16)
                        dve.tensor_copy(*pixels(n // 6, a, a + 2)).then_inc(regrouped_d, 1)
                dve.wait_ge(x_turned, n + 1)
                ph, nw = n // 6, n % 6
                dve.tensor_copy(patchesT[:, ph * 3:ph * 3 + 3, nw::GRID],
                                ps[:, n % 4, 0:288].rearrange("p (r n) -> p r n", r=3)).then_inc(x_kept_d, 1)

            def embed_tile(t):
                dve.wait_ge(embedded, t + 1)
                r = rows(t)
                step(dve.tensor_tensor(h[0:r, t, :], ps[0:r, 4 + t % 4, 0:D], pos_b[0:r, :], ALU.add))
                h_ready_now(t)

            def h_ready_now(t):
                r = rows(t)
                ins = dve.bn_stats(stats[0:r, t, :], h[0:r, t, :])
                ins.then_inc(h_ready, 1)
                dve.wait_ge(h_ready, t + 1)
                dve.bn_aggr(mv[0:r, t, :], stats[0:r, t, :]).then_inc(moments, 1)

            def norm_tile(t):
                r = rows(t)
                dve.wait_ge(rstd_ready, 1 + t // 3)
                dve.wait_ge(moments, t + 1)
                dve.tensor_scalar(xn[0:r, t, :], h[0:r, t, :], mv[0:r, t, 0:1], rstd[0:r, t:t + 1],
                                  ALU.subtract, ALU.mult).then_inc(xn_ready, 1)

            dve.wait_ge(zeros_ready, 4)
            for t in range(4):
                embed_tile(t)
            for t in range(3):
                norm_tile(t)
            for t in range(4, TT):
                embed_tile(t)
            for t in range(3, TT):
                norm_tile(t)
            dve.wait_ge(slots_scaled, 1)
            dve.tensor_scalar(slot_rows[0:S, :], slot_rows[0:S, :], slot_sc[0:S, 2:3], None,
                              ALU.mult).then_inc(slots_ready, 1)
            for bank in (4, 5):
                dve.memset(ps[32:64, bank, 0:OG * QW], 0.0).then_inc(junk_set, 1)

            def keep_k(half):
                for g in range(2):
                    dve.wait_ge(qk_done, half * 4 + g + 3)
                    dve.tensor_copy(kT[0:C2, g, half * HALF:(half + 1) * HALF],
                                    ps[0:C2, 2 + g, 0:HALF]).then_inc(k_ready, 1)

            keep_k(0)
            keep_k(1)
            dve.wait_ge(misc_kept, 2)
            for bank in (6, 7):
                dve.memset(ps[32:64, bank, 0:G3 * VW], 1.0).then_inc(junk_set, 1)
            dve.wait_ge(masks_ready, 1)

            def attn_tile(t, bank):
                r = rows(t)
                dve.wait_ge(attn_done, t + 1)
                dve.wait_ge(bias_added, t + 1)
                dve.tensor_tensor(h[0:r, t, :], ps[0:r, bank, 0:D], h[0:r, t, :], ALU.add).then_inc(h2_ready, 1)
                dve.wait_ge(h2_ready, t + 1)
                step(dve.bn_stats(stats[0:r, t, :], h[0:r, t, :]))
                dve.bn_aggr(mv[0:r, t, :], stats[0:r, t, :]).then_inc(moments2, 1)

            for i in range(PAIRS + 3):
                for t, bank in attn_tiles(i):
                    attn_tile(t, bank)
                if i < PAIRS:
                    sc = ps[0:R2, 4 + i % 2, 0:OG * QW].rearrange("p (h m) -> p h m", m=N)
                    dve.wait_ge(scores_ready, i + 1)
                    step(dve.tensor_reduce(mx[0:R2, i % 2, :], sc, AX.X, ALU.max))
                    if i >= 2:
                        dve.wait_ge(probs_turned, i - 1)
                    dve.tensor_tensor(probs[0:R2, i % 2, :].rearrange("p (h m) -> p h m", m=N), sc,
                                      mx[0:R2, i % 2, :].unsqueeze(2).to_broadcast([R2, HEADS, N]),
                                      ALU.subtract).then_inc(shifted, 1)
                    dve.wait_ge(v_done, i + 1)
                    if i >= 2:
                        dve.wait_ge(pv_done, i - 1)
                    dve.tensor_tensor(
                        v_diag[0:TR, i % 2, :, :].rearrange("p a (g w) -> p a g w", w=VW)[:, :, :, 0:3 * DH],
                        ps[0:TR, 2 + i % 2, 0:2 * D].rearrange("p (a g w) -> p a g w", a=2, g=G3),
                        value_mask[0:TR, :, :].unsqueeze(1).to_broadcast([TR, 2, G3, 3 * DH]),
                        ALU.mult).then_inc(vdiag_ready, 1)
                if 1 <= i <= PAIRS:
                    p = i - 1
                    o_ps = ps[0:R2, 6 + p % 2, 0:G3 * VW].rearrange("p (g w) -> p g w", w=VW)
                    dve.wait_ge(pv_done, p + 1)
                    step(dve.reciprocal(rcp[0:R2, p % 2, :].rearrange("p (g j) -> p g j", g=G3),
                                        o_ps[:, :, 3 * DH:VW]))
                    if p >= 2:
                        dve.wait_ge(o_turned, p - 1)
                    dve.tensor_tensor(
                        o_rows[0:R2, p % 2, :].rearrange("p (g j d) -> p g j d", g=G3, j=3),
                        o_ps[:, :, 0:3 * DH].rearrange("p g (j d) -> p g j d", j=3),
                        rcp[0:R2, p % 2, :].rearrange("p (g j) -> p g j", g=G3).unsqueeze(3)
                        .to_broadcast([R2, G3, 3, DH]), ALU.mult).then_inc(o_ready, 1)

            for bank in (6, 7):
                dve.memset(ps[:, bank, 0:TT * S], 0.0).then_inc(soft_banks, 1)
            dve.wait_ge(nw_in, 16)
            for a, b in ((0, 4), (4, TT)):
                for t in range(a, b):
                    r = rows(t)
                    step(dve.scalar_tensor_tensor(out=xn[0:r, t, :], in0=h[0:r, t, :], scalar=mv[0:r, t, 0:1],
                                                  in1=norm_row[0:r, :], op0=ALU.subtract, op1=ALU.mult))
                dve.wait_ge(scale2_ready, 1 if a == 0 else 2)
                for t in range(a, b):
                    r = rows(t)
                    dve.tensor_scalar(xn[0:r, t, :], xn[0:r, t, :], ln_scale[0:r, t:t + 1], None,
                                      ALU.mult).then_inc(xn2_ready, 1)
                if a == 0:
                    continue
                for t in range(TT):
                    r = rows(t)
                    dve.wait_ge(rnorm_ready, 1 if t < 4 else 2)
                    dve.wait_ge(xn2_ready, t + 1)
                    dve.tensor_scalar(tok[0:r, t, :], xn[0:r, t, :], rnorm[0:r, t:t + 1], None,
                                      ALU.mult).then_inc(tok_ready, 1)

            lg = logits[0:S, :].rearrange("p (b n) -> p b n", n=N)
            dg = disp[0:S, :].rearrange("p (b n) -> p b n", n=N)
            dve.wait_ge(logits_ready, 2)
            step(dve.tensor_reduce(soft[0:S, 0, :], lg, AX.X, ALU.max))
            dve.tensor_tensor(dg, lg, soft[0:S, 0, :].unsqueeze(2).to_broadcast([S, B, N]),
                              ALU.subtract).then_inc(d_shifted, 1)
            ct = ps[0:TR, 6, 0:TT * S].rearrange("p (t s) -> p t s", t=TT)
            dve.wait_ge(logits_turned, 1)
            step(dve.tensor_reduce(soft[0:TR, 1, 0:TT], ct, AX.X, ALU.max))
            dve.wait_ge(tok_turned, TT)
            dve.tensor_tensor(comb[0:TR, :, :], ct, soft[0:TR, 1, 0:TT].unsqueeze(2).to_broadcast([TR, TT, S]),
                              ALU.subtract).then_inc(c_shifted, 1)
            dve.wait_ge(d_exp, 1)
            step(dve.tensor_reduce(soft[0:S, 2, :], dg, AX.X, ALU.add))
            step(dve.reciprocal(soft[0:S, 3, :], soft[0:S, 2, :]))
            dve.tensor_tensor(dg, dg, soft[0:S, 3, :].unsqueeze(2).to_broadcast([S, B, N]),
                              ALU.mult).then_inc(disp_ready, 1)
            dve.wait_ge(disp_turned, 1)
            dve.tensor_tensor(disp_diag[0:TR],
                              ps[0:TR, 7, 0:TT * S].rearrange("p (t s) -> p t s", t=TT).unsqueeze(2)
                              .to_broadcast([TR, TT, TPI, S]),
                              image_mask[0:TR, :].unsqueeze(1).unsqueeze(3).to_broadcast([TR, TT, TPI, S]),
                              ALU.mult).then_inc(ddiag_ready, 1)
            dve.wait_ge(c_exp, 1)
            step(dve.tensor_reduce(soft[0:TR, 1, 8:8 + TT], comb[0:TR, :, :], AX.X, ALU.add))
            step(dve.reciprocal(soft[0:TR, 1, 0:TT], soft[0:TR, 1, 8:8 + TT]))
            dve.tensor_tensor(comb[0:TR, :, :], comb[0:TR, :, :],
                              soft[0:TR, 1, 0:TT].unsqueeze(2).to_broadcast([TR, TT, S]),
                              ALU.mult).then_inc(comb_ready, 1)
            for t in range(TT):
                n = min(TPI, B - TPI * t)
                dve.wait_ge(y_done, t + 1)
                if t == 0:
                    dve.wait_ge(ydiag_zero, 1)
                dve.tensor_copy(y_diag[0:64, :, :, TPI * t:TPI * t + n],
                                y_columns(0, t, n)
                                ).then_inc(y_kept_d, 1)
            step(dve.tensor_reduce(batch_mask[:, :], ident[:, :].rearrange("p (s b) -> p b s", b=B), AX.X, ALU.add))

            def mlp_group(g, gg, it):
                dve.wait_ge(mix_done, g + 1)
                earlier(dve, combined, g * 3)
                dve.tensor_tensor(mix[:, gg, :].rearrange("p (h b n) -> p h b n", h=2, n=N),
                                  ps[:, 2:4, 0:HALF].rearrange("p h (b n) -> p h b n", n=N),
                                  batch_mask[:, :].rearrange("p (h b) -> p h b", h=2).unsqueeze(3)
                                  .to_broadcast([128, 2, B // 2, N]), ALU.mult).then_inc(mix_ready, 1)
                dve.wait_ge(hid_turned, g + 1)
                earlier(dve, gact_ready, g * 2)
                for half in range(2):
                    dve.tensor_tensor(
                        pre[:, 3 * half:3 * half + 3, :].rearrange("p c (s b) -> p c s b", s=GS),
                        ps[:, 2 + half, 0:384].rearrange("p (c s b) -> p c s b", c=3, s=GS),
                        b1T[:, 3 * half:3 * half + 3, bass.ds(g * GS, GS)].unsqueeze(3)
                        .to_broadcast([128, 3, GS, B]), ALU.add).then_inc(pre_ready, 1)

            for gg in range(2):
                mlp_group(gg, gg, 0)
            with dve.Fori(1, GROUPS // 2) as it:
                for gg in range(2):
                    mlp_group(it * 2 + gg, gg, it)

            for tt in range(2):
                dve.wait_ge(combined, (GROUPS - 1) * 3 + tt + 1)
                dve.tensor_tensor(h[0:TR, 2 * tt:2 * tt + 2, :],
                                  ps[0:TR, 5 + tt, 0:2 * D].rearrange("p (t d) -> p t d", t=2),
                                  h[0:TR, 2 * tt:2 * tt + 2, :], ALU.add).then_inc(final_ready, 1)
            dve.wait_ge(combined, GROUPS * 3)
            for t in (TT - 2, TT - 1):
                dve.tensor_tensor(h[0:rows(t), t, :], ps[0:rows(t), 7, (t % 2) * D:(t % 2 + 1) * D],
                                  h[0:rows(t), t, :], ALU.add).then_inc(final_ready, 1)

        @block.tensor
        def _(pe):
            pe.wait_ge(ident_ready, 1)
            pe.wait_ge(wqkv_in, 16)
            for t in range(8):
                if t == 6:
                    pe.wait_ge(wproj_in, 16)
                if t >= 4:
                    pe.wait_ge(w_kept_d if t % 2 else w_kept_a, (t - 4) // 2 + 1)
                for c in range(2):
                    raw = qkv_raw[0:C2, t, c * C2:(c + 1) * C2] if t < 6 else proj_raw[0:C2, t - 6, c * C2:(c + 1) * C2]
                    mm = pe.transpose(ps[0:C2, 4 + t % 4, c * C2:(c + 1) * C2], raw, ident[0:C2, 0:C2])
                mm.then_inc(w_turned, 1)
            for n in range(12):
                ph, nw = n // 6, n % 6
                if nw < 4:
                    pe.wait_ge(regrouped_d, 2 * ph + nw // 2 + 1)
                else:
                    pe.wait_ge(regrouped_a, ph + 1)
                if n >= 4:
                    pe.wait_ge(x_kept_d if n % 2 else x_kept_a, (n - 4) // 2 + 1)
                for r in range(3):
                    mm = pe.transpose(ps[:, n % 4, r * C2:(r + 1) * C2],
                                      x_patch[0:C2, ph, nw, r * 128:(r + 1) * 128], ident[0:C2, 0:C2])
                mm.then_inc(x_turned, 1)
            pe.wait_ge(wp_in, 16)
            pe.wait_ge(x_kept_a, 6)
            pe.wait_ge(x_kept_d, 6)
            pe.wait_ge(w_kept_a, 4)
            pe.wait_ge(w_kept_d, 4)
            for t in range(TT):
                if t >= 4:
                    pe.wait_ge(h_ready, t - 3)
                for c in range(KC):
                    mm = pe.matmul(ps[0:rows(t), 4 + t % 4, 0:D], patchesT[:, c, t * TR:t * TR + rows(t)],
                                   embed_w[:, c, :], start=(c == 0), stop=(c == KC - 1))
                mm.then_inc(embedded, 1)
            pe.wait_ge(b1_in, 16)
            pe.wait_ge(h_ready, 3)
            b1v = b1_raw[0:S, :].rearrange("s (p c) -> s c p", c=FC)
            for c in range(FC):
                mm = pe.transpose(ps[:, 6, c * S:(c + 1) * S], b1v[:, c, :], ident[0:S, 0:S])
            mm.then_inc(misc_turned, 1)

            def turn_xn(t):
                pe.wait_ge(xn_ready, t + 1)
                if t >= 2:
                    pe.wait_ge(xT_ready, t - 1)
                r = rows(t)
                for c in range(2):
                    mm = pe.transpose(ps[0:C2, t % 2, c * r:(c + 1) * r], xn[0:r, t, c * C2:(c + 1) * C2],
                                      ident[0:r, 0:r])
                mm.then_inc(xn_turned, 1)

            def project_qk(half):
                pe.wait_ge(xT_ready, 3 if half == 0 else TT)
                for g in range(4):
                    if half or g >= 2:
                        n = half * 4 + g - 2
                        pe.wait_ge(q_ready if n % 4 < 2 else k_ready, n // 4 * 2 + n % 2 + 1)
                    for c in range(2):
                        mm = pe.matmul(ps[0:C2, 2 + g % 2, 0:HALF], qkvT[0:C2, c, g * C2:(g + 1) * C2],
                                       xT[0:C2, c, half * HALF:(half + 1) * HALF], start=(c == 0), stop=(c == 1))
                    mm.then_inc(qk_done, 1)

            for t in range(3):
                turn_xn(t)
            project_qk(0)
            for t in range(3, TT):
                turn_xn(t)
            project_qk(1)
            pe.wait_ge(slots_ready, 1)
            for c in range(2):
                mm = pe.transpose(ps[0:C2, 7, c * S:(c + 1) * S], slot_rows[0:S, c * C2:(c + 1) * C2], ident[0:S, 0:S])
            mm.then_inc(misc_turned, 1)

            for i in range(PAIRS + 3):
                for t, bank in attn_tiles(i):
                    r = rows(t)
                    pe.wait_ge(oT_ready, 2 * (i - 2))
                    if i > PAIRS:
                        pe.wait_ge(oT_ready, 2 * PAIRS)
                    for c in range(2):
                        mm = pe.matmul(ps[0:r, bank, 0:D], oT[0:C2, c, t * TR:t * TR + r], projT[0:C2, c, :],
                                       start=(c == 0), stop=(c == 1))
                    mm.then_inc(attn_done, 1)
                if i < PAIRS:
                    pe.wait_ge(kdiag_ready, 2 * (i + 1))
                    if i == 0:
                        pe.wait_ge(junk_set, 4)
                        pe.wait_ge(q_ready, 4)
                        pe.wait_ge(k_ready, 4)
                    else:
                        if i >= 2:
                            pe.wait_ge(shifted, i - 1)
                    for og in range(OG):
                        for a in range(2):
                            mm = pe.matmul(ps[64 * a:64 * a + N, 4 + i % 2, og * QW:(og + 1) * QW],
                                           qT[:, og, (2 * i + a) * N:(2 * i + a + 1) * N],
                                           k_diag[:, i % 2, og, a * QW:(a + 1) * QW], start=True, stop=True)
                    mm.then_inc(scores_ready, 1)
                if 1 <= i <= PAIRS:
                    p = i - 1
                    pe.wait_ge(exp_ready, p + 1)
                    if p >= 2:
                        pe.wait_ge(probsT_ready, p - 1)
                    for g in range(G3):
                        mm = pe.transpose(ps[0:TR, p % 2, g * R2:(g + 1) * R2],
                                          probs[0:R2, p % 2, g * TR:(g + 1) * TR], ident[0:R2, 0:R2])
                    mm.then_inc(probs_turned, 1)
                if i < PAIRS:
                    pe.wait_ge(copies_ready, 2 * (i + 1))
                    if i >= 2:
                        pe.wait_ge(vdiag_ready, i - 1)
                    for a in range(2):
                        for c in range(2):
                            mm = pe.matmul(ps[0:TR, 2 + i % 2, a * D:(a + 1) * D], x_copies[0:C2, i % 2, c, a, :],
                                           qkvT[0:C2, c, 2 * D:3 * D], start=(c == 0), stop=(c == 1))
                    mm.then_inc(v_done, 1)
                if 1 <= i <= PAIRS:
                    p = i - 1
                    pe.wait_ge(probsT_ready, p + 1)
                    pe.wait_ge(vdiag_ready, p + 1)
                    if p >= 2:
                        pe.wait_ge(oT_ready, 2 * (p - 1))
                    done = sum(len(attn_tiles(n)) for n in range(i + 1))
                    if done:
                        pe.wait_ge(h2_ready, done)
                    for g in range(G3):
                        for a in range(2):
                            mm = pe.matmul(ps[64 * a:64 * a + N, 6 + p % 2, g * VW:(g + 1) * VW],
                                           probsT[0:TR, p % 2, g, 64 * a:64 * a + N],
                                           v_diag[0:TR, p % 2, a, g * VW:(g + 1) * VW], start=True, stop=True)
                    mm.then_inc(pv_done, 1)
                if 2 <= i <= PAIRS + 1:
                    p = i - 2
                    pe.wait_ge(o_ready, p + 1)
                    for c in range(2):
                        mm = pe.transpose(ps[0:C2, 6 + p % 2, 256 + c * R2:256 + (c + 1) * R2],
                                          o_rows[0:R2, p % 2, c * C2:(c + 1) * C2], ident[0:R2, 0:R2])
                    mm.then_inc(o_turned, 1)

            def turn_tok(t):
                r = rows(t)
                pe.wait_ge(tok_ready, t + 1)
                if t >= 2:
                    pe.wait_ge(tokT_ready, t - 1)
                for c in range(2):
                    mm = pe.transpose(ps[0:C2, 2 + t % 2, c * r:(c + 1) * r], tok[0:r, t, c * C2:(c + 1) * C2],
                                      ident[0:r, 0:r])
                mm.then_inc(tok_turned, 1)

            for t in range(TT):
                turn_tok(t)
            pe.wait_ge(misc_kept, 2)
            for half in range(2):
                pe.wait_ge(tokT_ready, 3 if half == 0 else TT)
                for c in range(2):
                    mm = pe.matmul(ps[0:S, 4 + half, 0:HALF], slotT[0:C2, c, :],
                                   xT[0:C2, c, half * HALF:(half + 1) * HALF], start=(c == 0), stop=(c == 1))
                mm.then_inc(logits_done, 1)
            pe.wait_ge(logits_ready, 2)
            pe.wait_ge(soft_banks, 2)
            for t in range(TT):
                mm = pe.transpose(ps[0:rows(t), 6, t * S:(t + 1) * S], logits[0:S, t * TR:t * TR + rows(t)],
                                  ident[0:S, 0:S])
            mm.then_inc(logits_turned, 1)
            pe.wait_ge(disp_ready, 1)
            for t in range(TT):
                mm = pe.transpose(ps[0:rows(t), 7, t * S:(t + 1) * S], disp[0:S, t * TR:t * TR + rows(t)],
                                  ident[0:S, 0:S])
            mm.then_inc(disp_turned, 1)
            pe.wait_ge(ddiag_ready, 1)
            for t in range(TT):
                r, n = rows(t), min(TPI, B - TPI * t)
                if t >= 2:
                    pe.wait_ge(y_kept_d, t - 1)
                    pe.wait_ge(y_kept_a, t - 1)
                for j in range(3):
                    for l in range(2):
                        mm = pe.matmul(ps[64 * l:64 * l + 64, t % 2, j * 96:j * 96 + n * S // 2],
                                       xn[0:r, t, j::3],
                                       disp_diag[0:r, t, 0:n, :].rearrange("p b (q l) -> p b q l", l=2)[:, :, :, l],
                                       start=True, stop=True)
                mm.then_inc(y_done, 1)
            pe.wait_ge(comb_ready, 1)
            for t in range(TT):
                bank, col = (6, t * TR) if t < 4 else (7, (t - 4) * TR)
                mm = pe.transpose(ps[0:S, bank, col:col + rows(t)], comb[0:rows(t), t, :], ident[0:rows(t), 0:rows(t)])
                if t in (3, TT - 1):
                    mm.then_inc(comb_turned, 1)
            pe.wait_ge(combT_ready, 2)
            pe.wait_ge(b2_in, 16)
            pe.wait_ge(y_kept_d, TT)
            pe.wait_ge(y_kept_a, TT)
            for t in range(TT):
                r = rows(t)
                mm = pe.matmul(ps[0:r, 5 + t // 2, (t % 2) * D:(t % 2 + 1) * D], combT[0:S, t * TR:t * TR + r],
                               b2_rows[0:S, :], start=(t % 2 == 0), stop=False, skip_group_check=True)
            mm.then_inc(bias2_done, 1)

            def mlp_group(g, gg, it):
                pe.wait_ge(group_in, g * 2 + 2)
                earlier(pe, pre_ready, g * 2)
                for half in range(2):
                    mm = pe.matmul(ps[:, 2 + half, 0:HALF], sel[0:S, gg, :],
                                   combT[0:S, half * HALF:(half + 1) * HALF], start=True, stop=True)
                mm.then_inc(mix_done, 1)
                earlier(pe, hid_ready, g * 2)
                for j in range(3):
                    slot = gg * UNITS + j
                    pe.wait_ge(unit_in[slot], it * 16 + 16)
                    w = ring[:, slot, :].rearrange("p (q o) -> p q o", q=4)
                    for half in range(2):
                        for q in range(4):
                            mm = pe.matmul(ps[32 * q:32 * q + 32, half, 0:FF // 2],
                                           y_group[:, gg, j, 32 * q:32 * q + 32],
                                           w[:, q, half * FF // 2:(half + 1) * FF // 2],
                                           start=(j == 0), stop=(j == 2), tile_position=(0, 32 * q))
                    mm.then_inc(units_used, 1)
                pe.wait_ge(hid_ready, g * 2 + 2)
                pe.wait_ge(mix_ready, g + 1)
                for c in range(FC):
                    mm = pe.transpose(ps[:, 2 + c // 3, (c % 3) * 128:(c % 3 + 1) * 128], hid[:, c, :], ident[:, :])
                mm.then_inc(hid_turned, 1)
                pe.wait_ge(gact_ready, g * 2 + 2)
                earlier(pe, y2_ready, g)
                for u in range(3):
                    slot = gg * UNITS + 3 + u
                    pe.wait_ge(unit_in[slot], it * 16 + 16)
                    w = ring[:, slot, :].rearrange("p (s c d) -> p s c d", s=GS, c=2)
                    for cc in range(2):
                        for l in range(2):
                            for q in range(4):
                                first = u == 0 and cc == 0 and l == 0
                                last = u == 2 and cc == 1 and l == 1
                                mm = pe.matmul(ps[32 * q:32 * q + 32, 4, 0:D], gact[:, 2 * u + cc, 2 * q + l, :],
                                               w[:, 2 * q + l, cc, :], start=first, stop=last,
                                               tile_position=(0, 32 * q))
                    mm.then_inc(units_used, 1)
                pe.wait_ge(y2_ready, g + 1)
                for t in range(TT):
                    r = rows(t)
                    mm = pe.matmul(ps[0:r, 5 + t // 2, (t % 2) * D:(t % 2 + 1) * D],
                                   mix[:, gg, t * TR:t * TR + r], y2[:, gg, :],
                                   start=False, stop=False, skip_group_check=True)
                    if t % 2:
                        mm.then_inc(combined, 1)

            for gg in range(2):
                mlp_group(gg, gg, 0)
            with pe.Fori(1, GROUPS // 2) as it:
                for gg in range(2):
                    mlp_group(it * 2 + gg, gg, it)


_INS = ['x', 'L0_tok_W_proj', 'L0_tok_b_proj', 'L0_tok_pos_emb', 'L0_attn_w_qkv', 'L0_attn_w_proj',
        'L0_attn_b_proj', 'L0_ffn_slots', 'L0_ffn_scale', 'L0_ffn_fc1_weight', 'L0_ffn_fc1_bias',
        'L0_ffn_fc2_weight', 'L0_ffn_fc2_bias', 'L0_ffn_norm_weight']
_OUTS = [((16, 36, 192), 'float32')]


def kernel(**inputs):
    import numpy as _np
    import concourse.bacc as _bacc
    from concourse import mybir as _mybir
    from concourse.bass_utils import run_bass_kernel_spmd as _run

    nc = _bacc.Bacc("TRN2", target_bir_lowering=False, num_devices=1)
    arrays, args = {}, []
    for name in _INS:
        a = _np.ascontiguousarray(inputs[name])
        arrays[f"in_{name}_dram"] = a
        args.append(nc.dram_tensor(f"in_{name}_dram", a.shape, _mybir.dt.from_np(a.dtype), kind="ExternalInput").ap())
    for i, (shape, dtype) in enumerate(_OUTS):
        dt = _mybir.dt.from_np(_np.dtype(dtype))
        args.append(nc.dram_tensor(f"out_{i}_dram", shape, dt, kind="ExternalOutput").ap())
    vit_tower_kernel(nc, *args)
    r = _run(nc, [arrays], core_ids=[0])
    return r.results[0]["out_0_dram"]
```

```python
from contextlib import ExitStack

import concourse.bass as bass
from concourse import mybir

F32 = mybir.dt.float32
ALU = mybir.AluOpType
ACT = mybir.ActivationFunctionType
AX = mybir.AxisListType


def vit_tower_kernel(nc, x, tok_w, tok_b, tok_pos, w_qkv, w_proj, attn_b, slots, slot_scale,
                     fc1_w, fc1_b, fc2_w, fc2_b, norm_w, out):
    B, IMG, _, CH = x.shape
    KP, D = tok_w.shape
    N = tok_pos.shape[0]
    GRID = 6
    PATCH = IMG // GRID
    NT = B * N
    HEADS, DH = 12, 16
    S, _, FF = fc1_w.shape
    EPS = 1e-5
    TPI = 3
    TR = TPI * N
    TT = -(-B // TPI)
    HALF = NT // 2
    C2 = D // 2
    OG = 2
    HG = HEADS // OG
    G3 = HEADS // 3
    VW = 3 * DH + 3
    PAIRS = B // 2
    R2 = 64 + N
    QW = HG * N
    SCALE = DH ** -0.5
    GS = 8
    GROUPS = S // GS
    UNITS = 6
    RING = 2 * UNITS
    UF = GS * D * FF // 3 // 128
    FC = FF // 128
    KC = KP // 128
    XR = IMG * CH

    PART = ((0, 4 * TR), (4 * TR, NT))

    def rows(t):
        return min(TR, NT - TR * t)

    with ExitStack() as ctx:
        def sb(name, shape):
            return ctx.enter_context(nc.sbuf_tensor(name, shape, F32))

        def sem(name):
            return ctx.enter_context(nc.semaphore(name))

        ring = sb("ring", [128, RING, UF])
        EARLY = RING - 6
        early = ring[:, EARLY:RING, :].rearrange("p s n -> p (s n)")
        at = [0]

        def carve(base, *shape):
            n = 1
            for d in shape:
                n *= d
            v = base[:, at[0]:at[0] + n]
            at[0] += n
            if len(shape) == 2:
                v = v.rearrange("p (a b) -> p a b", a=shape[0])
            elif len(shape) == 3:
                v = v.rearrange("p (a b c) -> p a b c", a=shape[0], b=shape[1])
            elif len(shape) == 4:
                v = v.rearrange("p (a b c d) -> p a b c d", a=shape[0], b=shape[1], c=shape[2])
            return v

        x_rows = carve(early, 2, 8 * XR)
        x_patch = carve(early, 2, GRID, KP // 2)
        patchesT = carve(early, KC, NT)
        embed_w = carve(early, KC, D)
        qkv_raw = carve(early, 6, D)
        proj_raw = carve(early, 2, D)
        b1_raw = carve(early, FF)
        assert at[0] <= 6 * UF

        ident = sb("ident", [128, 128])
        h = sb("h", [128, TT, D])
        xn = sb("xn", [128, TT, D])
        xT = sb("xT", [128, 2, NT])
        qkvT = sb("qkvT", [128, 2, 3 * D])
        projT = sb("projT", [128, 2, D])
        pos_b = sb("pos_b", [128, D])
        attn_b_row = sb("attn_b_row", [128, D])
        norm_row = sb("norm_row", [128, D])
        slot_rows = sb("slot_rows", [128, D])
        slotT = sb("slotT", [128, 2, S])
        b1T = sb("b1T", [128, FC, S])
        b2_rows = sb("b2_rows", [128, D])
        head_mask = sb("head_mask", [128, HG])
        image_mask = sb("image_mask", [128, TPI])
        value_mask = sb("value_mask", [128, G3, 3 * DH])
        batch_mask = sb("batch_mask", [128, B])
        stats = sb("stats", [128, TT, 6])
        mv = sb("mv", [128, TT, 2])
        neg_half = sb("neg_half", [128, TT])
        rstd = sb("rstd", [128, TT])
        var_eps = sb("var_eps", [128, TT])
        floor = sb("floor", [128, TT])
        ln_scale = sb("ln_scale", [128, TT])
        ssq = sb("ssq", [128, TT])
        rnorm = sb("rnorm", [128, TT])
        slot_sc = sb("slot_sc", [128, 4])
        mx = sb("mx", [128, 2, HEADS])
        rcp = sb("rcp", [128, 2, HEADS])
        soft = sb("soft", [128, 4, B])
        soft_space = sb("soft_space", [128, 2 * NT])
        logits, disp = soft_space[:, 0:NT], soft_space[:, NT:2 * NT]
        x_copies = soft_space[:, 0:2 * 2 * 2 * TR].rearrange("p (i c a n) -> p i c a n", i=2, c=2, a=2)
        pos_raw, slot_squares = disp[:, 0:D], logits[:, 0:D]
        squares = slot_rows

        region_k = sb("region_k", [128, 4032])
        at[0] = 0
        qT = carve(region_k, OG, NT)
        kT = carve(region_k, OG, NT)
        k_diag = carve(region_k, 2, OG, 2 * QW)
        at[0] = 0
        y_diag = carve(region_k, 3, S // 2, 32)
        y2 = carve(region_k, 2, D)
        sel = carve(region_k, 2, 128)
        region_p = sb("region_p", [128, 3200])
        at[0] = 0
        probs = carve(region_p, 2, OG * QW)
        probsT = carve(region_p, 2, G3, R2)
        o_rows = carve(region_p, 2, D)
        oT = carve(region_p, 2, NT)
        at[0] = 0
        gact = carve(region_p, FC, GS, 32)
        hid = carve(region_p, FC, 128)
        pre = carve(region_p, FC, 128)
        v_diag = sb("v_diag", [128, 2, 2, G3 * VW])
        qkv_flat = qkvT[:, :, :].rearrange("p a b -> p (a b)")
        tok = qkv_flat[:, 0:TT * D].rearrange("p (t d) -> p t d", t=TT)
        comb = qkv_flat[:, 0:TT * S].rearrange("p (t s) -> p t s", t=TT)
        y_group = qkv_flat[:, TT * S:TT * S + 768].rearrange("p (g j n) -> p g j n", g=2, j=3)
        combT = v_diag[:, :, :, :].rearrange("p a b c -> p (a b c)")[:, 0:NT]
        disp_diag = region_p[:, 0:TT * TPI * S].rearrange("p (t i s) -> p t i s", t=TT, i=TPI)
        mix = soft_space[:, :].rearrange("p (g n) -> p g n", g=2)

        ps = ctx.enter_context(nc.psum_tensor("ps", [128, 8, 512], F32))

        wqkv_in, wproj_in, wp_in = sem("wqkv_in"), sem("wproj_in"), sem("wp_in")
        x_in = [sem("x_in0"), sem("x_in1")]
        pos_in, ab_in, nw_in = sem("pos_in"), sem("ab_in"), sem("nw_in")
        slots_in, b1_in, b2_in = sem("slots_in"), sem("b1_in"), sem("b2_in")
        unit_in = [sem(f"unit_in{i}") for i in range(RING)]
        units_used = sem("units_used")
        out_written = sem("out_written")
        ident_ready, masks_ready, zeros_ready = sem("ident_ready"), sem("masks_ready"), sem("zeros_ready")
        w_turned, w_kept = sem("w_turned"), sem("w_kept")
        regrouped_a, regrouped_d = sem("regrouped_a"), sem("regrouped_d")
        x_turned, x_kept_a, x_kept_d = sem("x_turned"), sem("x_kept_a"), sem("x_kept_d")
        embedded, h_ready, moments = sem("embedded"), sem("h_ready"), sem("moments")
        rstd_ready, xn_ready, bias_added = sem("rstd_ready"), sem("xn_ready"), sem("bias_added")
        slots_sq, slots_scaled, slots_ready = sem("slots_sq"), sem("slots_scaled"), sem("slots_ready")
        misc_turned, misc_kept = sem("misc_turned"), sem("misc_kept")
        xn_turned, xT_ready = sem("xn_turned"), sem("xT_ready")
        qk_done, q_ready, k_ready, kdiag_ready = sem("qk_done"), sem("q_ready"), sem("k_ready"), sem("kdiag_ready")
        copies_ready = sem("copies_ready")
        junk_set = sem("junk_set")
        scores_ready, shifted, exp_ready = sem("scores_ready"), sem("shifted"), sem("exp_ready")
        probs_turned, probsT_ready = sem("probs_turned"), sem("probsT_ready")
        v_done, vdiag_ready, pv_done = sem("v_done"), sem("vdiag_ready"), sem("pv_done")
        o_ready, o_turned, oT_ready = sem("o_ready"), sem("o_turned"), sem("oT_ready")
        centered = sem("centered")
        attn_done, h2_ready, moments2 = sem("attn_done"), sem("h2_ready"), sem("moments2")
        scale2_ready, xn2_ready, sq_ready, rnorm_ready = sem("scale2_ready"), sem("xn2_ready"), sem("sq_ready"), sem("rnorm_ready")
        tok_ready, tok_turned, tokT_ready = sem("tok_ready"), sem("tok_turned"), sem("tokT_ready")
        logits_done, logits_ready, soft_bank = sem("logits_done"), sem("logits_ready"), sem("soft_bank")
        logits_turned = sem("logits_turned")
        d_shifted, d_exp, disp_ready, disp_turned, ddiag_a_ready, ddiag_b_ready = (
            sem("d_shifted"), sem("d_exp"), sem("disp_ready"), sem("disp_turned"), sem("ddiag_a_ready"),
            sem("ddiag_b_ready"))
        c_shifted, c_exp, comb_ready, comb_turned, combT_ready = (
            sem("c_shifted"), sem("c_exp"), sem("comb_ready"), sem("comb_turned"), sem("combT_ready"))
        y_done, y_kept_d, y_kept_a = sem("y_done"), sem("y_kept_d"), sem("y_kept_a")
        ydiag_zero, gact_zero = sem("ydiag_zero"), sem("gact_zero")
        bias2_done = sem("bias2_done")
        group_in, sel_ready, mix_done, mix_ready = sem("group_in"), sem("sel_ready"), sem("mix_done"), sem("mix_ready")
        hid_ready, hid_turned = sem("hid_ready"), sem("hid_turned")
        pre_ready, gact_ready = sem("pre_ready"), sem("gact_ready")
        y2_ready, combined, final_ready = sem("y2_ready"), sem("combined"), sem("final_ready")
        dve_step, pool_step = sem("dve_step"), sem("pool_step")

        x_view = x.rearrange("b (n p) w c -> (b n) (p w c)", n=GRID)
        fc1_view = fc1_w.rearrange("s d o -> (s d) o").rearrange("(q p j) o -> j p q o", p=128, j=3)
        fc2_view = fc2_w.rearrange("s (p c) d -> p s c d", p=128)
        out_view = out.rearrange("b n d -> (b n) d")

        def attn_tiles(i):
            found = [t for t in range(TT) if min(TPI * t + TPI - 1, B - 1) // 2 == i - 3]
            return [(t, 6 + (i - 3 + n) % 2) for n, t in enumerate(found)]

        def y_columns(row, t, n):
            return ps[row:row + 64, (2 + t) % 4, 0:3 * 96].rearrange("p (j b q) -> p j q b", j=3, b=TPI)[:, :, :, 0:n]

        def pixels(ph, a, b):
            src = x_rows[0:C2, ph, :].rearrange("p (r w e) -> p w r e", r=8, w=GRID)[:, a:b]
            dst = x_patch[0:C2, ph, a:b, :].rearrange("p w (r e) -> p w r e", r=8)
            return dst, src

        def earlier(eng, signal, count):
            if not (isinstance(count, int) and count == 0):
                eng.wait_ge(signal, count)

        block = ctx.enter_context(nc.Block())

        @block.sync
        def _(sp):
            for ph in range(2):
                sp.dma_start(x_rows[0:C2, ph, :],
                             x_view[:, ph * 8 * XR:(ph + 1) * 8 * XR]).then_inc(x_in[ph], 16)
            sp.dma_start(embed_w[:, :, :], tok_w.rearrange("(c p) d -> p c d", p=128)).then_inc(wp_in, 16)
            for j in range(TPI):
                sp.dma_start(pos_raw[j * N:(j + 1) * N, :], tok_pos).then_inc(pos_in, 16)
            sp.dma_start(pos_b[0:TR, :], tok_b.partition_broadcast(TR)).then_inc(pos_in, 16)
            sp.dma_start(qkv_raw[0:C2], w_qkv.rearrange("(t p) c -> p t c", p=C2)).then_inc(wqkv_in, 16)
            sp.dma_start(proj_raw[0:C2], w_proj.rearrange("(t p) c -> p t c", p=C2)).then_inc(wproj_in, 16)
            sp.dma_start(slot_rows[0:S, :], slots).then_inc(slots_in, 16)
            sp.dma_start(slot_sc[0:S, 1:2], slot_scale.rearrange("(s a) -> s a", a=1)).then_inc(slots_in, 16)
            sp.dma_start(b1_raw[0:S, :], fc1_b).then_inc(b1_in, 16)
            sp.dma_start(attn_b_row[0:TR, :], attn_b.partition_broadcast(TR)).then_inc(ab_in, 16)
            sp.dma_start(norm_row[0:TR, :], norm_w.partition_broadcast(TR)).then_inc(nw_in, 16)
            sp.dma_start(b2_rows[0:S, :], fc2_b).then_inc(b2_in, 16)

            def load_unit(g, slot):
                u = slot % UNITS
                if u < 3:
                    dst = ring[:, slot, :].rearrange("p (q o) -> p q o", q=GS // 2)
                    src = fc1_view[u][:, bass.ds(g * (GS // 2), GS // 2), :]
                else:
                    dst = ring[:, slot, :].rearrange("p (s n) -> p s n", s=GS)
                    src = fc2_view[:, bass.ds(g * GS, GS), 2 * (u - 3):2 * (u - 3) + 2, :].rearrange(
                        "p s c d -> p s (c d)")
                sp.dma_start(dst, src).then_inc(unit_in[slot], 16)

            for slot in range(RING):
                if slot == EARLY:
                    sp.wait_ge(embedded, TT)
                    sp.wait_ge(misc_turned, 2)
                load_unit(slot // UNITS, slot)
            with sp.Fori(1, GROUPS // 2) as it:
                for slot in range(RING):
                    sp.wait_ge(units_used, it * RING + (slot + 1 - RING))
                    load_unit(it * 2 + slot // UNITS, slot)
            for tt in range(3):
                sp.wait_ge(final_ready, (1, 2, 4)[tt])
                if tt < 2:
                    sp.dma_start(out_view[2 * tt * TR:2 * (tt + 1) * TR, :].rearrange("(t p) d -> p t d", p=TR),
                                 h[0:TR, 2 * tt:2 * tt + 2, :]).then_inc(out_written, 16)
                else:
                    for t in (TT - 2, TT - 1):
                        sp.dma_start(out_view[t * TR:t * TR + rows(t), :],
                                     h[0:rows(t), t, :]).then_inc(out_written, 16)
            sp.wait_ge(out_written, 64)

        @block.gpsimd
        def _(pool):
            steps = [0]

            def step(ins):
                steps[0] += 1
                ins.then_inc(pool_step, 1)
                pool.wait_ge(pool_step, steps[0])

            step(pool.memset(ident[:, :], 0.0))
            step(pool.affine_select(out=ident[:, :], in_=ident[:, :], compare_op=ALU.not_equal, fill=1.0, base=0,
                                    pattern=[[-1, 128]], channel_multiplier=1))
            pool.memset(neg_half[:, :], -0.5).then_inc(ident_ready, 1)
            pool.wait_ge(ident_ready, 1)
            for n, (place, value) in enumerate(((mv[:, :, :], 1.0), (ssq[:, :], 1.0), (qT[96:128, :, :], 0.0),
                                                (k_diag[96:128, :, :, :], 0.0),
                                                (disp_diag[96:128, :, :, :], 0.0),
                                                (xn[96:128, :, :], 0.0))):
                pool.memset(place, value).then_inc(zeros_ready, 1)
                pool.wait_ge(zeros_ready, n + 1)

            def band(mask, pattern, width):
                step(pool.memset(mask, 1.0))
                step(pool.affine_select(out=mask, in_=mask, compare_op=ALU.is_ge, fill=0.0, base=0,
                                        pattern=[[-w, n] for w, n in pattern], channel_multiplier=1))
                step(pool.affine_select(out=mask, in_=mask, compare_op=ALU.is_ge, fill=0.0, base=width - 1,
                                        pattern=pattern, channel_multiplier=-1))

            band(head_mask[:, :], [[DH, HG]], DH)
            band(image_mask[:, :], [[N, TPI]], N)
            band(value_mask[:, :, :].rearrange("p g (j d) -> p g j d", j=3), [[0, G3], [N, 3], [0, DH]], N)
            v_blocks = v_diag[:, :, :, :].rearrange("p a b (g w) -> p (a b g) w", w=VW)
            pool.tensor_copy(v_blocks[0:TR, :, 3 * DH:VW],
                             image_mask[0:TR, :].unsqueeze(1).to_broadcast([TR, 16, 3])).then_inc(masks_ready, 1)

            for n in range(2):
                a, b = 3 * n, 3 * n + 3
                pool.wait_ge(moments, b)
                if n == 0:
                    pool.wait_ge(masks_ready, 1)
                step(pool.tensor_scalar(var_eps[:, a:b], mv[:, a:b, 1], EPS, None, ALU.add))
                pool.tensor_tensor(rstd[:, a:b], var_eps[:, a:b], neg_half[:, a:b], ALU.pow).then_inc(rstd_ready, 1)
            pool.wait_ge(slots_sq, 1)
            step(pool.tensor_scalar(slot_sc[0:S, 2:3], slot_sc[0:S, 0:1], EPS * EPS, None, ALU.max))
            step(pool.tensor_tensor(slot_sc[0:S, 3:4], slot_sc[0:S, 2:3], neg_half[0:S, 0:1], ALU.pow))
            pool.wait_ge(slots_in, 32)
            pool.tensor_tensor(slot_sc[0:S, 2:3], slot_sc[0:S, 3:4], slot_sc[0:S, 1:2],
                               ALU.mult).then_inc(slots_scaled, 1)

            def k_blocks(i):
                for og in range(OG):
                    pool.tensor_tensor(
                        k_diag[0:C2, i % 2, og, :].rearrange("p (a h m) -> p a h m", a=2, h=HG),
                        kT[0:C2, og, 2 * N * i:2 * N * (i + 1)].rearrange("p (a m) -> p a m", a=2)
                        .unsqueeze(2).to_broadcast([C2, 2, HG, N]),
                        head_mask[0:C2, :].unsqueeze(1).unsqueeze(3).to_broadcast([C2, 2, HG, N]),
                        ALU.mult).then_inc(kdiag_ready, 1)

            def ln_bias(i):
                if i == 0:
                    pool.wait_ge(ab_in, 16)
                pool.wait_ge(xn_ready, i + 1)
                pool.tensor_tensor(h[0:rows(i), i, :], h[0:rows(i), i, :], attn_b_row[0:rows(i), :],
                                   ALU.add).then_inc(bias_added, 1)

            def rms_scale(n):
                a, b = 2 * n, 2 * n + 2
                pool.wait_ge(moments2, b)
                step(pool.tensor_scalar(var_eps[:, a:b], mv[:, a:b, 1], 1.0 + EPS, EPS * EPS, ALU.mult, ALU.add))
                step(pool.tensor_scalar(floor[:, a:b], var_eps[:, a:b], EPS * EPS, None, ALU.mult))
                pool.tensor_tensor(ln_scale[:, a:b], var_eps[:, a:b], neg_half[:, a:b],
                                   ALU.pow).then_inc(scale2_ready, 1)

            def rms_norms(n):
                for t in (2 * n, 2 * n + 1):
                    pool.wait_ge(sq_ready, t + 1)
                    step(pool.tensor_scalar(ssq[:, t:t + 1], ssq[:, t:t + 1], floor[:, t:t + 1], None, ALU.max))
                    pool.tensor_tensor(rnorm[:, t:t + 1], ssq[:, t:t + 1], neg_half[:, t:t + 1],
                                       ALU.pow).then_inc(rnorm_ready, 1)

            for i in range(PAIRS):
                pool.wait_ge(k_ready, 2 if i < 4 else 4)
                if i >= 2:
                    pool.wait_ge(scores_ready, i - 1)
                k_blocks(i)
                if i < TT:
                    ln_bias(i)

            rms_scale(0)
            rms_norms(0)
            pool.wait_ge(scores_ready, PAIRS)
            pool.memset(y_diag[:, :, :, :], 0.0).then_inc(ydiag_zero, 1)
            pool.wait_ge(ydiag_zero, 1)
            rms_scale(1)

            def select(g, gg):
                pool.tensor_copy(sel[0:S, gg, :].rearrange("p (s b) -> p s b", s=GS),
                                 ident[0:S, bass.ds(g * GS, GS)].unsqueeze(2).to_broadcast([S, GS, B])
                                 ).then_inc(sel_ready, 1)

            rms_norms(1)
            select(0, 0)
            rms_scale(2)
            rms_norms(2)
            select(1, 1)
            pool.wait_ge(y_done, TT)
            pool.memset(gact[:, :, :, :], 0.0).then_inc(gact_zero, 1)

            pool.wait_ge(y_kept_d, TT)
            pool.wait_ge(y_kept_a, TT)
            with pool.Fori(1, GROUPS // 2) as it:
                for gg in range(2):
                    g = it * 2 + gg
                    pool.wait_ge(units_used, g * UNITS + (3 - 2 * UNITS))
                    pool.tensor_copy(y_group[:, gg, :, :].rearrange("p j (q n) -> p j q n", q=4),
                                     y_diag[:, :, bass.ds(g * 4, 4), :]).then_inc(group_in, 1)
                    pool.wait_ge(mix_done, g - 1)
                    select(g, gg)

        @block.scalar
        def _(act):
            for n in range(0, 12, 2):
                if n % 6 == 0:
                    act.wait_ge(x_in[n // 6], 16)
                    act.copy(*pixels(n // 6, 4, 6)).then_inc(regrouped_a, 1)
                act.wait_ge(x_turned, n + 1)
                ph, nw = n // 6, n % 6
                act.copy(patchesT[:, ph * 3:ph * 3 + 3, nw::GRID],
                         ps[:, n % 4, 0:288].rearrange("p (r n) -> p r n", r=3)).then_inc(x_kept_a, 1)
            for t in range(8):
                act.wait_ge(w_turned, t + 1)
                dst = qkvT[0:C2, :, t * C2:(t + 1) * C2] if t < 6 else projT[0:C2, :, (t - 6) * C2:(t - 5) * C2]
                act.copy(dst, ps[0:C2, t % 4, 0:2 * C2].rearrange("p (c n) -> p c n", c=2)).then_inc(w_kept, 1)
            act.wait_ge(slots_in, 32)
            act.activation(slot_squares[0:S, :], slot_rows[0:S, :], ACT.Square,
                           accum_out=slot_sc[0:S, 0:1]).then_inc(slots_sq, 1)

            def keep_xT(t):
                act.wait_ge(xn_turned, t + 1)
                act.copy(xT[0:C2, :, t * TR:t * TR + rows(t)],
                         ps[0:C2, t % 2, 0:2 * rows(t)].rearrange("p (c n) -> p c n", c=2)).then_inc(xT_ready, 1)

            def keep_q(half):
                for g in range(2):
                    act.wait_ge(qk_done, half * 4 + g + 1)
                    act.mul(qT[0:C2, g, half * HALF:(half + 1) * HALF],
                            ps[0:C2, 2 + g, 0:HALF], SCALE).then_inc(q_ready, 1)

            for t in range(3):
                keep_xT(t)
            act.wait_ge(misc_turned, 1)
            act.copy(b1T[:, :, :], ps[:, 6, 0:FC * S].rearrange("p (c s) -> p c s", c=FC)).then_inc(misc_kept, 1)
            keep_q(0)
            for t in range(3, TT):
                keep_xT(t)
            keep_q(1)
            act.wait_ge(misc_turned, 2)
            act.copy(slotT[0:C2, :, :], ps[0:C2, 7, 0:2 * S].rearrange("p (c s) -> p c s", c=2)).then_inc(misc_kept, 1)

            def copy_tokens(i):
                if i >= 2:
                    act.wait_ge(v_done, i - 1)
                for c in range(2):
                    act.copy(x_copies[0:C2, i % 2, c, :, :].rearrange("p a (j n) -> p a j n", j=3),
                             xT[0:C2, c, 2 * N * i:2 * N * (i + 1)].rearrange("p (a n) -> p a n", a=2)
                             .unsqueeze(2).to_broadcast([C2, 2, 3, N])).then_inc(copies_ready, 1)

            def square(t):
                if t:
                    act.wait_ge(sq_ready, t)
                act.wait_ge(centered, t + 1)
                act.activation(squares[0:rows(t), :], xn[0:rows(t), t, :], ACT.Square,
                               accum_out=ssq[0:rows(t), t:t + 1]).then_inc(sq_ready, 1)

            def keep_tokT(t):
                act.wait_ge(tok_turned, t + 1)
                act.copy(xT[0:C2, :, t * TR:t * TR + rows(t)],
                         ps[0:C2, 2 + t % 2, 0:2 * rows(t)].rearrange("p (c n) -> p c n", c=2)).then_inc(tokT_ready, 1)

            for t in range(TT):
                act.wait_ge(xT_ready, t + 1)
            copy_tokens(0)
            for i in range(PAIRS + 3):
                if 1 <= i <= PAIRS:
                    act.wait_ge(probs_turned, i)
                    if i >= 3:
                        act.wait_ge(pv_done, i - 2)
                    act.copy(probsT[0:TR, (i - 1) % 2, :, :],
                             ps[0:TR, (i - 1) % 2, 0:G3 * R2].rearrange("p (g n) -> p g n", g=G3)
                             ).then_inc(probsT_ready, 1)
                if i < PAIRS:
                    act.wait_ge(shifted, i + 1)
                    act.activation(probs[0:R2, i % 2, :], probs[0:R2, i % 2, :], ACT.Exp).then_inc(exp_ready, 1)
                if i + 1 < PAIRS:
                    copy_tokens(i + 1)
                if 2 <= i <= PAIRS + 1:
                    p = i - 2
                    act.wait_ge(o_turned, p + 1)
                    src = ps[0:C2, 6 + p % 2, 256:256 + 2 * R2].rearrange("p (c n) -> p c n", c=2)
                    for a in range(2):
                        cp = act.copy(oT[0:C2, :, (2 * p + a) * N:(2 * p + a + 1) * N], src[:, :, 64 * a:64 * a + N])
                        cp.then_inc(oT_ready, 1)
                for t in {6: (0, 1), 8: (2,), 9: (3,)}.get(i, ()):
                    square(t)
            for t in (0, 1):
                keep_tokT(t)
            square(4)
            square(5)
            for t in range(2, 4):
                keep_tokT(t)

            def keep_logits(part):
                act.wait_ge(logits_done, part + 1)
                a, b = PART[part]
                act.copy(logits[0:S, a:b], ps[0:S, 4 + part, 0:b - a]).then_inc(logits_ready, 1)

            def exp_dispatch(part):
                act.wait_ge(d_shifted, part + 1)
                a, b = PART[part]
                act.activation(disp[0:S, a:b], disp[0:S, a:b], ACT.Exp).then_inc(d_exp, 1)

            for t in range(4, TT):
                keep_tokT(t)
            exp_dispatch(0)
            exp_dispatch(1)
            act.wait_ge(disp_turned, 1)
            for i in range(TPI):
                act.mul(disp_diag[0:TR, 0:4, i, :], ps[0:TR, 7, 0:4 * S].rearrange("p (t s) -> p t s", t=4),
                        image_mask[0:TR, i:i + 1]).then_inc(ddiag_a_ready, 1)
            keep_logits(0)
            keep_logits(1)
            for t in range(TT):
                n = min(TPI, B - TPI * t)
                act.wait_ge(y_done, t + 1)
                if t == 0:
                    act.wait_ge(ydiag_zero, 1)
                act.copy(y_diag[64:128, :, :, B + TPI * t:B + TPI * t + n],
                         y_columns(64, t, n)
                         ).then_inc(y_kept_a, 1)

            def mlp_group(g, gg, it):
                static = isinstance(g, int)
                if static and g == 0:
                    act.wait_ge(c_shifted, 1)
                    act.activation(comb[0:TR, :, :], comb[0:TR, :, :], ACT.Exp).then_inc(c_exp, 1)
                act.wait_ge(units_used, g * UNITS + 3)
                earlier(act, hid_turned, g)
                for half in range(2):
                    act.copy(hid[:, :, half * 64:(half + 1) * 64].rearrange("p c n -> p n c"),
                             ps[:, half, 0:FF // 2].rearrange("p (n c) -> p n c", c=FC)).then_inc(hid_ready, 1)
                if static and g == 0:
                    act.wait_ge(comb_turned, 1)
                    act.copy(combT[0:S, 0:4 * TR], ps[0:S, 7, 0:4 * TR]).then_inc(combT_ready, 1)
                    act.wait_ge(comb_turned, 2)
                    act.copy(combT[0:S, 4 * TR:NT], ps[0:S, 4, 0:NT - 4 * TR]).then_inc(combT_ready, 1)
                    act.wait_ge(gact_zero, 1)
                act.wait_ge(pre_ready, g * 2 + 2)
                earlier(act, units_used, g * UNITS)
                gflat = gact[:, :, :, :].rearrange("p c s n -> p (c s n)").rearrange("p (k n) -> p k n", n=64)
                src = pre[:, :, :].rearrange("p c (q l b) -> p (c q) l b", l=2, b=B)
                for l in range(2):
                    act.activation(gflat[:, :, 48 * l:48 * l + B], src[:, :, l, :], ACT.Gelu).then_inc(gact_ready, 1)
                act.wait_ge(units_used, g * UNITS + 6)
                act.copy(y2[:, gg, :], ps[:, 4, 0:D]).then_inc(y2_ready, 1)

            for gg in range(2):
                mlp_group(gg, gg, 0)
            with act.Fori(1, GROUPS // 2) as it:
                for gg in range(2):
                    mlp_group(it * 2 + gg, gg, it)

        @block.vector
        def _(dve):
            steps = [0]

            def step(ins):
                steps[0] += 1
                ins.then_inc(dve_step, 1)
                dve.wait_ge(dve_step, steps[0])

            for n in range(1, 12, 2):
                if n % 6 == 1:
                    for a in (0, 2):
                        dve.wait_ge(x_in[n // 6], 16)
                        dve.tensor_copy(*pixels(n // 6, a, a + 2)).then_inc(regrouped_d, 1)
                dve.wait_ge(x_turned, n + 1)
                ph, nw = n // 6, n % 6
                dve.tensor_copy(patchesT[:, ph * 3:ph * 3 + 3, nw::GRID],
                                ps[:, n % 4, 0:288].rearrange("p (r n) -> p r n", r=3)).then_inc(x_kept_d, 1)

            def embed_tile(t):
                dve.wait_ge(embedded, t + 1)
                r = rows(t)
                step(dve.tensor_tensor(h[0:r, t, :], ps[0:r, 4 + t % 4, 0:D], pos_b[0:r, :], ALU.add))
                h_ready_now(t)

            def h_ready_now(t):
                r = rows(t)
                ins = dve.bn_stats(stats[0:r, t, :], h[0:r, t, :])
                ins.then_inc(h_ready, 1)
                dve.wait_ge(h_ready, t + 1)
                dve.bn_aggr(mv[0:r, t, :], stats[0:r, t, :]).then_inc(moments, 1)

            def norm_tile(t):
                r = rows(t)
                dve.wait_ge(rstd_ready, 1 + t // 3)
                dve.wait_ge(moments, t + 1)
                dve.tensor_scalar(xn[0:r, t, :], h[0:r, t, :], mv[0:r, t, 0:1], rstd[0:r, t:t + 1],
                                  ALU.subtract, ALU.mult).then_inc(xn_ready, 1)

            dve.wait_ge(pos_in, 64)
            step(dve.tensor_tensor(pos_b[0:TR, :], pos_b[0:TR, :], pos_raw[0:TR, :], ALU.add))
            dve.wait_ge(zeros_ready, 6)
            for t in range(4):
                embed_tile(t)
            for t in range(3):
                norm_tile(t)
            for t in range(4, TT):
                embed_tile(t)
            for t in range(3, TT):
                norm_tile(t)
            step(dve.tensor_reduce(batch_mask[:, :], ident[:, :].rearrange("p (s b) -> p b s", b=B), AX.X, ALU.add))
            dve.wait_ge(slots_scaled, 1)
            dve.tensor_scalar(slot_rows[0:S, :], slot_rows[0:S, :], slot_sc[0:S, 2:3], None,
                              ALU.mult).then_inc(slots_ready, 1)
            for bank in (4, 5):
                dve.memset(ps[32:64, bank, 0:OG * QW], 0.0).then_inc(junk_set, 1)

            def keep_k(half):
                for g in range(2):
                    dve.wait_ge(qk_done, half * 4 + g + 3)
                    dve.tensor_copy(kT[0:C2, g, half * HALF:(half + 1) * HALF],
                                    ps[0:C2, 2 + g, 0:HALF]).then_inc(k_ready, 1)

            keep_k(0)
            keep_k(1)
            dve.wait_ge(misc_kept, 2)
            for bank in (6, 7):
                dve.memset(ps[32:64, bank, 0:G3 * VW], 1.0).then_inc(junk_set, 1)
            dve.wait_ge(masks_ready, 1)

            def attn_tile(t, bank):
                r = rows(t)
                dve.wait_ge(attn_done, t + 1)
                dve.wait_ge(bias_added, t + 1)
                dve.tensor_tensor(h[0:r, t, :], ps[0:r, bank, 0:D], h[0:r, t, :], ALU.add).then_inc(h2_ready, 1)
                dve.wait_ge(h2_ready, t + 1)
                step(dve.bn_stats(stats[0:r, t, :], h[0:r, t, :]))
                dve.bn_aggr(mv[0:r, t, :], stats[0:r, t, :]).then_inc(moments2, 1)

            def center(t):
                r = rows(t)
                if t == 0:
                    dve.wait_ge(nw_in, 16)
                dve.wait_ge(moments2, t + 1)
                dve.scalar_tensor_tensor(out=xn[0:r, t, :], in0=h[0:r, t, :], scalar=mv[0:r, t, 0:1],
                                         in1=norm_row[0:r, :], op0=ALU.subtract, op1=ALU.mult).then_inc(centered, 1)

            def unit_token(t):
                dve.wait_ge(rnorm_ready, t + 1)
                dve.wait_ge(centered, t + 1)
                dve.tensor_scalar(tok[0:rows(t), t, :], xn[0:rows(t), t, :], rnorm[0:rows(t), t:t + 1], None,
                                  ALU.mult).then_inc(tok_ready, 1)

            def scale_rms(t):
                dve.wait_ge(scale2_ready, t // 2 + 1)
                dve.tensor_scalar(xn[0:rows(t), t, :], xn[0:rows(t), t, :], ln_scale[0:rows(t), t:t + 1], None,
                                  ALU.mult).then_inc(xn2_ready, 1)

            for i in range(PAIRS + 3):
                if i < PAIRS:
                    sc = ps[0:R2, 4 + i % 2, 0:OG * QW].rearrange("p (h m) -> p h m", m=N)
                    dve.wait_ge(scores_ready, i + 1)
                    step(dve.tensor_reduce(mx[0:R2, i % 2, :], sc, AX.X, ALU.max))
                    if i >= 2:
                        dve.wait_ge(probs_turned, i - 1)
                    dve.tensor_tensor(probs[0:R2, i % 2, :].rearrange("p (h m) -> p h m", m=N), sc,
                                      mx[0:R2, i % 2, :].unsqueeze(2).to_broadcast([R2, HEADS, N]),
                                      ALU.subtract).then_inc(shifted, 1)
                for t, bank in attn_tiles(i):
                    attn_tile(t, bank)
                    if i == PAIRS + 2:
                        center(t)
                        if t == 4:
                            unit_token(2)
                            unit_token(3)
                if i < PAIRS:
                    dve.wait_ge(v_done, i + 1)
                    if i >= 2:
                        dve.wait_ge(pv_done, i - 1)
                    dve.tensor_tensor(
                        v_diag[0:TR, i % 2, :, :].rearrange("p a (g w) -> p a g w", w=VW)[:, :, :, 0:3 * DH],
                        ps[0:TR, 2 + i % 2, 0:2 * D].rearrange("p (a g w) -> p a g w", a=2, g=G3),
                        value_mask[0:TR, :, :].unsqueeze(1).to_broadcast([TR, 2, G3, 3 * DH]),
                        ALU.mult).then_inc(vdiag_ready, 1)
                if 1 <= i <= PAIRS:
                    p = i - 1
                    o_ps = ps[0:R2, 6 + p % 2, 0:G3 * VW].rearrange("p (g w) -> p g w", w=VW)
                    dve.wait_ge(pv_done, p + 1)
                    step(dve.reciprocal(rcp[0:R2, p % 2, :].rearrange("p (g j) -> p g j", g=G3),
                                        o_ps[:, :, 3 * DH:VW]))
                    if p >= 2:
                        dve.wait_ge(o_turned, p - 1)
                    dve.tensor_tensor(
                        o_rows[0:R2, p % 2, :].rearrange("p (g j d) -> p g j d", g=G3, j=3),
                        o_ps[:, :, 0:3 * DH].rearrange("p g (j d) -> p g j d", j=3),
                        rcp[0:R2, p % 2, :].rearrange("p (g j) -> p g j", g=G3).unsqueeze(3)
                        .to_broadcast([R2, G3, 3, DH]), ALU.mult).then_inc(o_ready, 1)
                if i < PAIRS + 2:
                    for t, bank in attn_tiles(i):
                        center(t)
                if i == PAIRS + 1:
                    for t in (0, 1):
                        unit_token(t)
                    for t in (0, 1):
                        scale_rms(t)
            for t in (2, 3):
                scale_rms(t)
            for t in (4, 5):
                unit_token(t)

            def keep_mix(g, gg):
                dve.wait_ge(mix_done, g + 1)
                dve.tensor_tensor(mix[:, gg, :].rearrange("p (h b n) -> p h b n", h=2, n=N),
                                  ps[:, 0:2, 0:HALF].rearrange("p h (b n) -> p h b n", n=N),
                                  batch_mask[:, :].rearrange("p (h b) -> p h b", h=2).unsqueeze(3)
                                  .to_broadcast([128, 2, B // 2, N]), ALU.mult).then_inc(mix_ready, 1)

            def shift_dispatch(part):
                a, b = PART[part]
                lg = ps[0:S, 4 + part, 0:b - a].rearrange("p (b n) -> p b n", n=N)
                dg = disp[0:S, a:b].rearrange("p (b n) -> p b n", n=N)
                a, b = a // N, b // N
                dve.wait_ge(logits_done, part + 1)
                step(dve.tensor_reduce(soft[0:S, 0, a:b], lg, AX.X, ALU.max))
                dve.tensor_tensor(dg, lg, soft[0:S, 0, a:b].unsqueeze(2).to_broadcast([S, b - a, N]),
                                  ALU.subtract).then_inc(d_shifted, 1)

            def normalise_dispatch(part):
                a, b = PART[part]
                dg = disp[0:S, a:b].rearrange("p (b n) -> p b n", n=N)
                a, b = a // N, b // N
                dve.wait_ge(d_exp, part + 1)
                step(dve.tensor_reduce(soft[0:S, 2, a:b], dg, AX.X, ALU.add))
                step(dve.reciprocal(soft[0:S, 3, a:b], soft[0:S, 2, a:b]))
                dve.tensor_tensor(dg, dg, soft[0:S, 3, a:b].unsqueeze(2).to_broadcast([S, b - a, N]),
                                  ALU.mult).then_inc(disp_ready, 1)

            shift_dispatch(0)
            for t in (4, 5):
                scale_rms(t)
            shift_dispatch(1)
            normalise_dispatch(0)
            normalise_dispatch(1)
            dve.wait_ge(disp_turned, 2)
            dve.tensor_tensor(disp_diag[0:TR, 4],
                              ps[0:TR, 6, 0:S].unsqueeze(1).to_broadcast([TR, TPI, S]),
                              image_mask[0:TR, :].unsqueeze(2).to_broadcast([TR, TPI, S]),
                              ALU.mult).then_inc(ddiag_b_ready, 1)
            dve.tensor_copy(disp_diag[0:N, 5, 0, :], ps[0:N, 6, S:2 * S]).then_inc(ddiag_b_ready, 1)
            for t in range(TT):
                n = min(TPI, B - TPI * t)
                dve.wait_ge(y_done, t + 1)
                if t == 0:
                    dve.wait_ge(ydiag_zero, 1)
                dve.tensor_copy(y_diag[0:64, :, :, TPI * t:TPI * t + n],
                                y_columns(0, t, n)
                                ).then_inc(y_kept_d, 1)
            dve.wait_ge(ddiag_a_ready, TPI)
            dve.memset(ps[:, 7, (TT - 1) * S:TT * S], 0.0).then_inc(soft_bank, 1)
            ct = ps[0:TR, 7, 0:TT * S].rearrange("p (t s) -> p t s", t=TT)
            dve.wait_ge(logits_turned, 1)
            step(dve.tensor_reduce(soft[0:TR, 1, 0:TT], ct, AX.X, ALU.max))
            dve.wait_ge(tok_turned, TT)
            dve.tensor_tensor(comb[0:TR, :, :], ct, soft[0:TR, 1, 0:TT].unsqueeze(2).to_broadcast([TR, TT, S]),
                              ALU.subtract).then_inc(c_shifted, 1)
            dve.wait_ge(c_exp, 1)
            step(dve.tensor_reduce(soft[0:TR, 1, 8:8 + TT], comb[0:TR, :, :], AX.X, ALU.add))
            step(dve.reciprocal(soft[0:TR, 1, 0:TT], soft[0:TR, 1, 8:8 + TT]))
            dve.tensor_tensor(comb[0:TR, :, :], comb[0:TR, :, :],
                              soft[0:TR, 1, 0:TT].unsqueeze(2).to_broadcast([TR, TT, S]),
                              ALU.mult).then_inc(comb_ready, 1)

            def mlp_group(g, gg, it):
                dve.wait_ge(hid_turned, g + 1)
                earlier(dve, gact_ready, g * 2)
                for half in range(2):
                    dve.tensor_tensor(
                        pre[:, 3 * half:3 * half + 3, :].rearrange("p c (s b) -> p c s b", s=GS),
                        ps[:, 2 + half, 0:384].rearrange("p (c s b) -> p c s b", c=3, s=GS),
                        b1T[:, 3 * half:3 * half + 3, bass.ds(g * GS, GS)].unsqueeze(3)
                        .to_broadcast([128, 3, GS, B]), ALU.add).then_inc(pre_ready, 1)
                keep_mix(g, gg)

            for gg in range(2):
                mlp_group(gg, gg, 0)
            with dve.Fori(1, GROUPS // 2) as it:
                for gg in range(2):
                    mlp_group(it * 2 + gg, gg, it)

            for tt in range(2):
                dve.wait_ge(combined, (GROUPS - 1) * 3 + tt + 1)
                dve.tensor_tensor(h[0:TR, 2 * tt:2 * tt + 2, :],
                                  ps[0:TR, 5 + tt, 0:2 * D].rearrange("p (t d) -> p t d", t=2),
                                  h[0:TR, 2 * tt:2 * tt + 2, :], ALU.add).then_inc(final_ready, 1)
            dve.wait_ge(combined, GROUPS * 3)
            for t in (TT - 2, TT - 1):
                dve.tensor_tensor(h[0:rows(t), t, :], ps[0:rows(t), 7, (t % 2) * D:(t % 2 + 1) * D],
                                  h[0:rows(t), t, :], ALU.add).then_inc(final_ready, 1)

        @block.tensor
        def _(pe):
            pe.wait_ge(ident_ready, 1)
            for n in range(12):
                ph, nw = n // 6, n % 6
                if nw < 4:
                    pe.wait_ge(regrouped_d, 2 * ph + nw // 2 + 1)
                else:
                    pe.wait_ge(regrouped_a, ph + 1)
                if n >= 4:
                    pe.wait_ge(x_kept_d if n % 2 else x_kept_a, (n - 4) // 2 + 1)
                for r in range(3):
                    mm = pe.transpose(ps[:, n % 4, r * C2:(r + 1) * C2],
                                      x_patch[0:C2, ph, nw, r * 128:(r + 1) * 128], ident[0:C2, 0:C2])
                mm.then_inc(x_turned, 1)
            pe.wait_ge(wp_in, 16)
            pe.wait_ge(x_kept_a, 6)
            pe.wait_ge(x_kept_d, 6)

            def embed(t):
                if t >= 4:
                    pe.wait_ge(h_ready, t - 3)
                for c in range(KC):
                    mm = pe.matmul(ps[0:rows(t), 4 + t % 4, 0:D], patchesT[:, c, t * TR:t * TR + rows(t)],
                                   embed_w[:, c, :], start=(c == 0), stop=(c == KC - 1))
                mm.then_inc(embedded, 1)

            def turn_weights(a, b):
                for t in range(a, b):
                    pe.wait_ge(wqkv_in if t < 6 else wproj_in, 16)
                    if t >= 4:
                        pe.wait_ge(w_kept, t - 3)
                    for c in range(2):
                        cols = slice(c * C2, (c + 1) * C2)
                        raw = qkv_raw[0:C2, t, cols] if t < 6 else proj_raw[0:C2, t - 6, cols]
                        mm = pe.transpose(ps[0:C2, t % 4, cols], raw, ident[0:C2, 0:C2])
                    mm.then_inc(w_turned, 1)

            def turn_xn(t):
                pe.wait_ge(xn_ready, t + 1)
                if t >= 2:
                    pe.wait_ge(xT_ready, t - 1)
                r = rows(t)
                for c in range(2):
                    mm = pe.transpose(ps[0:C2, t % 2, c * r:(c + 1) * r], xn[0:r, t, c * C2:(c + 1) * C2],
                                      ident[0:r, 0:r])
                mm.then_inc(xn_turned, 1)

            def project_qk(half):
                pe.wait_ge(xT_ready, 3 if half == 0 else TT)
                for g in range(4):
                    if half or g >= 2:
                        n = half * 4 + g - 2
                        pe.wait_ge(q_ready if n % 4 < 2 else k_ready, n // 4 * 2 + n % 2 + 1)
                    for c in range(2):
                        mm = pe.matmul(ps[0:C2, 2 + g % 2, 0:HALF], qkvT[0:C2, c, g * C2:(g + 1) * C2],
                                       xT[0:C2, c, half * HALF:(half + 1) * HALF], start=(c == 0), stop=(c == 1))
                    mm.then_inc(qk_done, 1)

            embed(0)
            embed(1)
            turn_weights(0, 4)
            embed(2)
            embed(3)
            turn_weights(4, 8)
            embed(4)
            pe.wait_ge(w_kept, 8)
            for t in range(3):
                turn_xn(t)
            embed(5)
            pe.wait_ge(b1_in, 16)
            pe.wait_ge(h_ready, 3)
            b1v = b1_raw[0:S, :].rearrange("s (p c) -> s c p", c=FC)
            for c in range(FC):
                mm = pe.transpose(ps[:, 6, c * S:(c + 1) * S], b1v[:, c, :], ident[0:S, 0:S])
            mm.then_inc(misc_turned, 1)
            project_qk(0)
            for t in range(3, TT):
                turn_xn(t)
            project_qk(1)
            pe.wait_ge(slots_ready, 1)
            for c in range(2):
                mm = pe.transpose(ps[0:C2, 7, c * S:(c + 1) * S], slot_rows[0:S, c * C2:(c + 1) * C2], ident[0:S, 0:S])
            mm.then_inc(misc_turned, 1)

            for i in range(PAIRS + 3):
                if i < PAIRS:
                    pe.wait_ge(kdiag_ready, 2 * (i + 1))
                    if i == 0:
                        pe.wait_ge(junk_set, 4)
                        pe.wait_ge(q_ready, 4)
                        pe.wait_ge(k_ready, 4)
                    else:
                        if i >= 2:
                            pe.wait_ge(shifted, i - 1)
                    for og in range(OG):
                        for a in range(2):
                            mm = pe.matmul(ps[64 * a:64 * a + N, 4 + i % 2, og * QW:(og + 1) * QW],
                                           qT[:, og, (2 * i + a) * N:(2 * i + a + 1) * N],
                                           k_diag[:, i % 2, og, a * QW:(a + 1) * QW], start=True, stop=True)
                    mm.then_inc(scores_ready, 1)
                if 1 <= i <= PAIRS:
                    p = i - 1
                    pe.wait_ge(exp_ready, p + 1)
                    if p >= 2:
                        pe.wait_ge(probsT_ready, p - 1)
                    for g in range(G3):
                        mm = pe.transpose(ps[0:TR, p % 2, g * R2:(g + 1) * R2],
                                          probs[0:R2, p % 2, g * TR:(g + 1) * TR], ident[0:R2, 0:R2])
                    mm.then_inc(probs_turned, 1)
                for t, bank in attn_tiles(i):
                    r = rows(t)
                    pe.wait_ge(oT_ready, 2 * (i - 2))
                    if i > PAIRS:
                        pe.wait_ge(oT_ready, 2 * PAIRS)
                    for c in range(2):
                        mm = pe.matmul(ps[0:r, bank, 0:D], oT[0:C2, c, t * TR:t * TR + r], projT[0:C2, c, :],
                                       start=(c == 0), stop=(c == 1))
                    mm.then_inc(attn_done, 1)
                if i < PAIRS:
                    pe.wait_ge(copies_ready, 2 * (i + 1))
                    if i >= 2:
                        pe.wait_ge(vdiag_ready, i - 1)
                    for a in range(2):
                        for c in range(2):
                            mm = pe.matmul(ps[0:TR, 2 + i % 2, a * D:(a + 1) * D], x_copies[0:C2, i % 2, c, a, :],
                                           qkvT[0:C2, c, 2 * D:3 * D], start=(c == 0), stop=(c == 1))
                    mm.then_inc(v_done, 1)
                if 1 <= i <= PAIRS:
                    p = i - 1
                    pe.wait_ge(probsT_ready, p + 1)
                    pe.wait_ge(vdiag_ready, p + 1)
                    if p >= 2:
                        pe.wait_ge(oT_ready, 2 * (p - 1))
                    done = sum(len(attn_tiles(n)) for n in range(i + 1))
                    if done:
                        pe.wait_ge(h2_ready, done)
                    for g in range(G3):
                        for a in range(2):
                            mm = pe.matmul(ps[64 * a:64 * a + N, 6 + p % 2, g * VW:(g + 1) * VW],
                                           probsT[0:TR, p % 2, g, 64 * a:64 * a + N],
                                           v_diag[0:TR, p % 2, a, g * VW:(g + 1) * VW], start=True, stop=True)
                    mm.then_inc(pv_done, 1)
                if 2 <= i <= PAIRS + 1:
                    p = i - 2
                    pe.wait_ge(o_ready, p + 1)
                    for c in range(2):
                        mm = pe.transpose(ps[0:C2, 6 + p % 2, 256 + c * R2:256 + (c + 1) * R2],
                                          o_rows[0:R2, p % 2, c * C2:(c + 1) * C2], ident[0:R2, 0:R2])
                    mm.then_inc(o_turned, 1)

            def turn_tok(t):
                r = rows(t)
                pe.wait_ge(tok_ready, t + 1)
                if t >= 2:
                    pe.wait_ge(tokT_ready, t - 1)
                for c in range(2):
                    mm = pe.transpose(ps[0:C2, 2 + t % 2, c * r:(c + 1) * r], tok[0:r, t, c * C2:(c + 1) * C2],
                                      ident[0:r, 0:r])
                mm.then_inc(tok_turned, 1)

            def logit_sums(part):
                a, b = PART[part]
                pe.wait_ge(tokT_ready, 4 if part == 0 else TT)
                for c in range(2):
                    mm = pe.matmul(ps[0:S, 4 + part, 0:b - a], slotT[0:C2, c, :], xT[0:C2, c, a:b],
                                   start=(c == 0), stop=(c == 1))
                mm.then_inc(logits_done, 1)

            def turn_dispatch(part, bank):
                pe.wait_ge(disp_ready, part + 1)
                pe.wait_ge(h2_ready, TT)
                tiles = range(4) if part == 0 else range(4, TT)
                for n, t in enumerate(tiles):
                    mm = pe.transpose(ps[0:rows(t), bank, n * S:(n + 1) * S], disp[0:S, t * TR:t * TR + rows(t)],
                                      ident[0:S, 0:S])
                mm.then_inc(disp_turned, 1)

            def slot_inputs(t):
                if t < 4:
                    pe.wait_ge(ddiag_a_ready, TPI)
                else:
                    pe.wait_ge(ddiag_b_ready, 2)
                    pe.wait_ge(y_kept_d, t - 3)
                    pe.wait_ge(y_kept_a, t - 3)
                pe.wait_ge(xn2_ready, t + 1)
                r, n = 128 if t < TT - 1 else rows(t), min(TPI, B - TPI * t)
                for j in range(3):
                    for l in range(2):
                        mm = pe.matmul(ps[64 * l:64 * l + 64, (2 + t) % 4, j * 96:j * 96 + n * S // 2],
                                       xn[0:r, t, j::3],
                                       disp_diag[0:r, t, 0:n, :].rearrange("p b (q l) -> p b q l", l=2)[:, :, :, l],
                                       start=True, stop=True)
                mm.then_inc(y_done, 1)

            for t in range(4):
                turn_tok(t)
            pe.wait_ge(misc_kept, 2)
            logit_sums(0)
            for t in range(4, TT):
                turn_tok(t)
            logit_sums(1)
            turn_dispatch(0, 7)
            turn_dispatch(1, 6)
            for t in range(TT):
                slot_inputs(t)
            pe.wait_ge(logits_ready, 2)
            pe.wait_ge(soft_bank, 1)
            for t in range(TT):
                mm = pe.transpose(ps[0:rows(t), 7, t * S:(t + 1) * S], logits[0:S, t * TR:t * TR + rows(t)],
                                  ident[0:S, 0:S])
            mm.then_inc(logits_turned, 1)
            pe.wait_ge(y_kept_d, TT)
            pe.wait_ge(y_kept_a, TT)

            def turn_combine():
                pe.wait_ge(comb_ready, 1)
                for t in range(TT):
                    bank, col = (7, t * TR) if t < 4 else (4, (t - 4) * TR)
                    mm = pe.transpose(ps[0:S, bank, col:col + rows(t)], comb[0:rows(t), t, :],
                                      ident[0:rows(t), 0:rows(t)])
                    if t in (3, TT - 1):
                        mm.then_inc(comb_turned, 1)

            def open_output(t):
                r = rows(t)
                pe.matmul(ps[0:r, 5 + t // 2, (t % 2) * D:(t % 2 + 1) * D], combT[0:S, t * TR:t * TR + r],
                          b2_rows[0:S, :], start=(t % 2 == 0), stop=False, skip_group_check=True)

            def mix_weights(g, gg):
                pe.wait_ge(sel_ready, g + 1)
                for half in range(2):
                    mm = pe.matmul(ps[:, half, 0:HALF], sel[0:S, gg, :],
                                   combT[0:S, half * HALF:(half + 1) * HALF], start=True, stop=True)
                mm.then_inc(mix_done, 1)

            def combine(g, gg):
                pe.wait_ge(y2_ready, g + 1)
                pe.wait_ge(mix_ready, g + 1)
                for t in range(TT):
                    r = rows(t)
                    mm = pe.matmul(ps[0:r, 5 + t // 2, (t % 2) * D:(t % 2 + 1) * D],
                                   mix[:, gg, t * TR:t * TR + r], y2[:, gg, :],
                                   start=False, stop=False, skip_group_check=True)
                    if t % 2:
                        mm.then_inc(combined, 1)

            def mlp_group(g, gg, it):
                static = isinstance(g, int)
                earlier(pe, mix_ready, g)
                if not static:
                    pe.wait_ge(group_in, g - 1)
                for j in range(3):
                    slot = gg * UNITS + j
                    pe.wait_ge(unit_in[slot], it * 16 + 16)
                    w = ring[:, slot, :].rearrange("p (q o) -> p q o", q=4)
                    for half in range(2):
                        for q in range(4):
                            y = y_diag[:, j, 4 * g + q, :] if static else y_group[:, gg, j, 32 * q:32 * q + 32]
                            mm = pe.matmul(ps[32 * q:32 * q + 32, half, 0:FF // 2], y,
                                           w[:, q, half * FF // 2:(half + 1) * FF // 2],
                                           start=(j == 0), stop=(j == 2), tile_position=(0, 32 * q))
                    mm.then_inc(units_used, 1)
                if static and g == 0:
                    turn_combine()
                else:
                    combine(g - 1, 1 - gg)
                pe.wait_ge(hid_ready, g * 2 + 2)
                earlier(pe, pre_ready, g * 2)
                for c in range(FC):
                    mm = pe.transpose(ps[:, 2 + c // 3, (c % 3) * 128:(c % 3 + 1) * 128], hid[:, c, :], ident[:, :])
                mm.then_inc(hid_turned, 1)
                if static and g == 0:
                    pe.wait_ge(combT_ready, 2)
                    pe.wait_ge(b2_in, 16)
                    for t in range(TT):
                        open_output(t)
                mix_weights(g, gg)
                pe.wait_ge(gact_ready, g * 2 + 2)
                earlier(pe, y2_ready, g)
                for u in range(3):
                    slot = gg * UNITS + 3 + u
                    pe.wait_ge(unit_in[slot], it * 16 + 16)
                    w = ring[:, slot, :].rearrange("p (s c d) -> p s c d", s=GS, c=2)
                    for cc in range(2):
                        for l in range(2):
                            for q in range(4):
                                first = u == 0 and cc == 0 and l == 0
                                last = u == 2 and cc == 1 and l == 1
                                mm = pe.matmul(ps[32 * q:32 * q + 32, 4, 0:D], gact[:, 2 * u + cc, 2 * q + l, :],
                                               w[:, 2 * q + l, cc, :], start=first, stop=last,
                                               tile_position=(0, 32 * q))
                    mm.then_inc(units_used, 1)

            for gg in range(2):
                mlp_group(gg, gg, 0)
            with pe.Fori(1, GROUPS // 2) as it:
                for gg in range(2):
                    mlp_group(it * 2 + gg, gg, it)
            combine(GROUPS - 1, 1)


_INS = ['x', 'L0_tok_W_proj', 'L0_tok_b_proj', 'L0_tok_pos_emb', 'L0_attn_w_qkv', 'L0_attn_w_proj',
        'L0_attn_b_proj', 'L0_ffn_slots', 'L0_ffn_scale', 'L0_ffn_fc1_weight', 'L0_ffn_fc1_bias',
        'L0_ffn_fc2_weight', 'L0_ffn_fc2_bias', 'L0_ffn_norm_weight']
_OUTS = [((16, 36, 192), 'float32')]


def kernel(**inputs):
    import numpy as _np
    import concourse.bacc as _bacc
    from concourse import mybir as _mybir
    from concourse.bass_utils import run_bass_kernel_spmd as _run

    nc = _bacc.Bacc("TRN2", target_bir_lowering=False, num_devices=1)
    arrays, args = {}, []
    for name in _INS:
        a = _np.ascontiguousarray(inputs[name])
        arrays[f"in_{name}_dram"] = a
        args.append(nc.dram_tensor(f"in_{name}_dram", a.shape, _mybir.dt.from_np(a.dtype), kind="ExternalInput").ap())
    for i, (shape, dtype) in enumerate(_OUTS):
        dt = _mybir.dt.from_np(_np.dtype(dtype))
        args.append(nc.dram_tensor(f"out_{i}_dram", shape, dt, kind="ExternalOutput").ap())
    vit_tower_kernel(nc, *args)
    r = _run(nc, [arrays], core_ids=[0])
    return r.results[0]["out_0_dram"]
```

```python
from contextlib import ExitStack

import concourse.bass as bass
from concourse import mybir

F32 = mybir.dt.float32
ALU = mybir.AluOpType
ACT = mybir.ActivationFunctionType
AX = mybir.AxisListType


def vit_tower_kernel(nc, x, tok_w, tok_b, tok_pos, w_qkv, w_proj, attn_b, slots, slot_scale,
                     fc1_w, fc1_b, fc2_w, fc2_b, norm_w, out):
    B, IMG, _, CH = x.shape
    KP, D = tok_w.shape
    N = tok_pos.shape[0]
    GRID = 6
    PATCH = IMG // GRID
    NT = B * N
    HEADS, DH = 12, 16
    S, _, FF = fc1_w.shape
    EPS = 1e-5
    TPI = 3
    TR = TPI * N
    TT = -(-B // TPI)
    HALF = NT // 2
    C2 = D // 2
    OG = 2
    HG = HEADS // OG
    G3 = HEADS // 3
    VW = 3 * DH + 3
    PAIRS = B // 2
    R2 = 64 + N
    QW = HG * N
    SCALE = DH ** -0.5
    GS = 8
    GROUPS = S // GS
    UNITS = 6
    RING = 2 * UNITS
    UF = GS * D * FF // 3 // 128
    FC = FF // 128
    KC = KP // 128
    XR = IMG * CH

    PARTS = 3

    def rows(t):
        return min(TR, NT - TR * t)

    def span(part):
        return 2 * part * TR, min(NT, 2 * (part + 1) * TR)

    with ExitStack() as ctx:
        def sb(name, shape):
            return ctx.enter_context(nc.sbuf_tensor(name, shape, F32))

        def sem(name):
            return ctx.enter_context(nc.semaphore(name))

        ring = sb("ring", [128, RING, UF])
        EARLY = RING - UNITS
        early = ring[:, EARLY:RING, :].rearrange("p s n -> p (s n)")
        at = [0]

        def carve(base, *shape):
            n = 1
            for d in shape:
                n *= d
            v = base[:, at[0]:at[0] + n]
            at[0] += n
            if len(shape) == 2:
                v = v.rearrange("p (a b) -> p a b", a=shape[0])
            elif len(shape) == 3:
                v = v.rearrange("p (a b c) -> p a b c", a=shape[0], b=shape[1])
            elif len(shape) == 4:
                v = v.rearrange("p (a b c d) -> p a b c d", a=shape[0], b=shape[1], c=shape[2])
            return v

        x_rows = carve(early, 2, 8 * XR)
        x_patch = carve(early, 2, GRID, KP // 2)
        patchesT = carve(early, KC, NT)
        embed_w = carve(early, KC, D)
        qkv_raw = carve(early, 6, D)
        proj_raw = carve(early, 2, D)
        b1_raw = carve(early, FF)
        assert at[0] <= (RING - EARLY) * UF

        ident = sb("ident", [128, 128])
        h = sb("h", [128, TT, D])
        xn = sb("xn", [128, TT, D])
        xT = sb("xT", [128, 2, NT])
        qkvT = sb("qkvT", [128, 2, 3 * D])
        projT = sb("projT", [128, 2, D])
        pos_b = sb("pos_b", [128, D])
        attn_b_row = sb("attn_b_row", [128, D])
        norm_row = sb("norm_row", [128, D])
        slot_rows = sb("slot_rows", [128, D])
        slotT = sb("slotT", [128, 2, S])
        b1T = sb("b1T", [128, FC, S])
        b2_rows = sb("b2_rows", [128, D])
        head_mask = sb("head_mask", [128, HG])
        image_mask = sb("image_mask", [128, TPI])
        value_mask = sb("value_mask", [128, G3, 3 * DH])
        batch_mask = sb("batch_mask", [128, B])
        stats = sb("stats", [128, TT, 6])
        mv = sb("mv", [128, TT, 2])
        neg_half = sb("neg_half", [128, TT])
        rstd = sb("rstd", [128, TT])
        var_eps = sb("var_eps", [128, TT])
        floor = sb("floor", [128, TT])
        ln_scale = sb("ln_scale", [128, TT])
        ssq = sb("ssq", [128, TT])
        rnorm = sb("rnorm", [128, TT])
        slot_sc = sb("slot_sc", [128, 4])
        mx = sb("mx", [128, 2, HEADS])
        rcp = sb("rcp", [128, 2, HEADS])
        soft = sb("soft", [128, 4, B])
        soft_space = sb("soft_space", [128, 2 * NT])
        logits, disp = soft_space[:, 0:NT], soft_space[:, NT:2 * NT]
        x_copies = soft_space[:, 0:2 * 2 * 2 * TR].rearrange("p (i c a n) -> p i c a n", i=2, c=2, a=2)
        pos_raw, slot_squares = disp[:, 0:D], logits[:, 0:D]
        squares = slot_rows

        region_k = sb("region_k", [128, 4032])
        at[0] = 0
        qT = carve(region_k, OG, NT)
        kT = carve(region_k, OG, NT)
        k_diag = carve(region_k, 2, OG, 2 * QW)
        at[0] = 0
        y_diag = carve(region_k, 3, S // 2, 32)
        y2 = carve(region_k, 2, D)
        sel = carve(region_k, 2, 128)
        region_p = sb("region_p", [128, 3200])
        at[0] = 0
        probs = carve(region_p, 2, OG * QW)
        probsT = carve(region_p, 2, G3, R2)
        o_rows = carve(region_p, 2, D)
        oT = carve(region_p, 2, NT)
        at[0] = 0
        gact = carve(region_p, FC, GS, 32)
        hid = carve(region_p, FC, 128)
        pre = carve(region_p, FC, 128)
        v_diag = sb("v_diag", [128, 2, 2, G3 * VW])
        qkv_flat = qkvT[:, :, :].rearrange("p a b -> p (a b)")
        tok = qkv_flat[:, 0:TT * D].rearrange("p (t d) -> p t d", t=TT)
        comb = qkv_flat[:, 0:TT * S].rearrange("p (t s) -> p t s", t=TT)
        y_group = qkv_flat[:, TT * S:TT * S + 2 * 3 * 128].rearrange("p (g j n) -> p g j n", g=2, j=3)
        combT = v_diag[:, :, :, :].rearrange("p a b c -> p (a b c)")[:, 0:NT]
        disp_diag = region_p[:, 0:TT * TPI * S].rearrange("p (t i s) -> p t i s", t=TT, i=TPI)
        mix = soft_space[:, :].rearrange("p (g n) -> p g n", g=2)

        ps = ctx.enter_context(nc.psum_tensor("ps", [128, 8, 512], F32))

        wqkv_in, wproj_in, wp_in = sem("wqkv_in"), sem("wproj_in"), sem("wp_in")
        x_in = [sem("x_in0"), sem("x_in1")]
        pos_in, ab_in, nw_in = sem("pos_in"), sem("ab_in"), sem("nw_in")
        slots_in, b1_in, b2_in = sem("slots_in"), sem("b1_in"), sem("b2_in")
        unit_in = [sem(f"unit_in{i}") for i in range(RING)]
        units_used = sem("units_used")
        out_written = sem("out_written")
        ident_ready, masks_ready, zeros_ready = sem("ident_ready"), sem("masks_ready"), sem("zeros_ready")
        w_turned, w_kept = sem("w_turned"), sem("w_kept")
        regrouped_a, regrouped_d = sem("regrouped_a"), sem("regrouped_d")
        x_turned, x_kept_a, x_kept_d = sem("x_turned"), sem("x_kept_a"), sem("x_kept_d")
        embedded, h_ready, moments = sem("embedded"), sem("h_ready"), sem("moments")
        rstd_ready, xn_ready, bias_added = sem("rstd_ready"), sem("xn_ready"), sem("bias_added")
        slots_sq, slots_scaled, slots_ready = sem("slots_sq"), sem("slots_scaled"), sem("slots_ready")
        misc_turned, misc_kept = sem("misc_turned"), sem("misc_kept")
        xn_turned, xT_ready = sem("xn_turned"), sem("xT_ready")
        qk_done, q_ready, k_ready, kdiag_ready = sem("qk_done"), sem("q_ready"), sem("k_ready"), sem("kdiag_ready")
        copies_ready = sem("copies_ready")
        junk_set = sem("junk_set")
        scores_ready, shifted, exp_ready = sem("scores_ready"), sem("shifted"), sem("exp_ready")
        probs_turned, probsT_ready = sem("probs_turned"), sem("probsT_ready")
        v_done, vdiag_ready, pv_done = sem("v_done"), sem("vdiag_ready"), sem("pv_done")
        o_ready, o_turned, oT_ready = sem("o_ready"), sem("o_turned"), sem("oT_ready")
        centered = sem("centered")
        attn_done, h2_ready, moments2 = sem("attn_done"), sem("h2_ready"), sem("moments2")
        floor_ready, floored = sem("floor_ready"), sem("floored")
        scale2_ready, sq_ready, rnorm_ready = sem("scale2_ready"), sem("sq_ready"), sem("rnorm_ready")
        tok_ready, tok_turned, tokT_ready = sem("tok_ready"), sem("tok_turned"), sem("tokT_ready")
        logits_done, logits_ready, soft_bank = sem("logits_done"), sem("logits_ready"), sem("soft_bank")
        logits_turned = sem("logits_turned")
        d_shifted, d_exp, disp_ready, disp_turned, ddiag_ready = (
            sem("d_shifted"), sem("d_exp"), sem("disp_ready"), sem("disp_turned"),
            sem("ddiag_ready"))
        c_shifted, c_exp, comb_ready, comb_turned, combT_ready = (
            sem("c_shifted"), sem("c_exp"), sem("comb_ready"), sem("comb_turned"), sem("combT_ready"))
        y_done, y_kept_d, y_kept_a = sem("y_done"), sem("y_kept_d"), sem("y_kept_a")
        ydiag_zero, gact_zero = sem("ydiag_zero"), sem("gact_zero")
        group_in, sel_ready, mix_done, mix_ready = sem("group_in"), sem("sel_ready"), sem("mix_done"), sem("mix_ready")
        hid_ready, hid_turned = sem("hid_ready"), sem("hid_turned")
        pre_ready, gact_ready = sem("pre_ready"), sem("gact_ready")
        y2_ready, combined, final_ready = sem("y2_ready"), sem("combined"), sem("final_ready")
        dve_step, pool_step = sem("dve_step"), sem("pool_step")

        x_view = x.rearrange("b (n p) w c -> (b n) (p w c)", n=GRID)
        fc1_view = fc1_w.rearrange("s d o -> (s d) o").rearrange("(q p j) o -> j p q o", p=128, j=3)
        fc2_view = fc2_w.rearrange("s (p c) d -> p s c d", p=128)
        out_view = out.rearrange("b n d -> (b n) d")

        def attn_tiles(i):
            found = [t for t in range(TT) if min(TPI * t + TPI - 1, B - 1) // 2 == i - 3]
            return [(t, 6 + (i - 3) % 2 if i < PAIRS else 4 + (t + 1) % 2) for t in found]

        def y_columns(row, t, n):
            return ps[row:row + 64, 3 + t % 3, 0:3 * 96].rearrange("p (j b q) -> p j q b", j=3, b=TPI)[:, :, :, 0:n]

        def pixels(ph, a, b):
            src = x_rows[0:C2, ph, :].rearrange("p (r w e) -> p w r e", r=8, w=GRID)[:, a:b]
            dst = x_patch[0:C2, ph, a:b, :].rearrange("p w (r e) -> p w r e", r=8)
            return dst, src

        def earlier(eng, signal, count):
            if not (isinstance(count, int) and count == 0):
                eng.wait_ge(signal, count)

        block = ctx.enter_context(nc.Block())

        @block.sync
        def _(sp):
            for ph in range(2):
                sp.dma_start(x_rows[0:C2, ph, :],
                             x_view[:, ph * 8 * XR:(ph + 1) * 8 * XR]).then_inc(x_in[ph], 16)
                if ph == 0:
                    sp.dma_start(embed_w[:, :, :], tok_w.rearrange("(c p) d -> p c d", p=128)).then_inc(wp_in, 16)
            for j in range(TPI):
                sp.dma_start(pos_raw[j * N:(j + 1) * N, :], tok_pos).then_inc(pos_in, 16)
            sp.dma_start(pos_b[0:TR, :], tok_b.partition_broadcast(TR)).then_inc(pos_in, 16)
            sp.dma_start(qkv_raw[0:C2], w_qkv.rearrange("(t p) c -> p t c", p=C2)).then_inc(wqkv_in, 16)
            sp.dma_start(proj_raw[0:C2], w_proj.rearrange("(t p) c -> p t c", p=C2)).then_inc(wproj_in, 16)
            sp.dma_start(slot_rows[0:S, :], slots).then_inc(slots_in, 16)
            sp.dma_start(slot_sc[0:S, 1:2], slot_scale.rearrange("(s a) -> s a", a=1)).then_inc(slots_in, 16)
            sp.dma_start(b1_raw[0:S, :], fc1_b).then_inc(b1_in, 16)
            sp.dma_start(attn_b_row[0:TR, :], attn_b.partition_broadcast(TR)).then_inc(ab_in, 16)
            sp.dma_start(norm_row[0:TR, :], norm_w.partition_broadcast(TR)).then_inc(nw_in, 16)
            sp.dma_start(b2_rows[0:S, :], fc2_b).then_inc(b2_in, 16)

            def load_unit(g, slot):
                u = slot % UNITS
                if u < 3:
                    dst = ring[:, slot, :].rearrange("p (q o) -> p q o", q=GS // 2)
                    src = fc1_view[u][:, bass.ds(g * (GS // 2), GS // 2), :]
                else:
                    dst = ring[:, slot, :].rearrange("p (s n) -> p s n", s=GS)
                    src = fc2_view[:, bass.ds(g * GS, GS), 2 * (u - 3):2 * (u - 3) + 2, :].rearrange(
                        "p s c d -> p s (c d)")
                sp.dma_start(dst, src).then_inc(unit_in[slot], 16)

            for slot in range(RING):
                if slot == EARLY:
                    sp.wait_ge(embedded, TT)
                    sp.wait_ge(misc_turned, 2)
                load_unit(slot // UNITS, slot)
            with sp.Fori(1, GROUPS // 2) as it:
                for slot in range(RING):
                    sp.wait_ge(units_used, it * RING + (slot + 1 - RING))
                    load_unit(it * 2 + slot // UNITS, slot)
            for tt in range(3):
                sp.wait_ge(final_ready, (1, 2, 4)[tt])
                if tt < 2:
                    sp.dma_start(out_view[2 * tt * TR:2 * (tt + 1) * TR, :].rearrange("(t p) d -> p t d", p=TR),
                                 h[0:TR, 2 * tt:2 * tt + 2, :]).then_inc(out_written, 16)
                else:
                    for t in (TT - 2, TT - 1):
                        sp.dma_start(out_view[t * TR:t * TR + rows(t), :],
                                     h[0:rows(t), t, :]).then_inc(out_written, 16)
            sp.wait_ge(out_written, 64)

        @block.gpsimd
        def _(pool):
            steps = [0]

            def step(ins):
                steps[0] += 1
                ins.then_inc(pool_step, 1)
                pool.wait_ge(pool_step, steps[0])

            step(pool.memset(ident[:, :], 0.0))
            step(pool.affine_select(out=ident[:, :], in_=ident[:, :], compare_op=ALU.not_equal, fill=1.0, base=0,
                                    pattern=[[-1, 128]], channel_multiplier=1))
            pool.memset(neg_half[:, :], -0.5).then_inc(ident_ready, 1)
            pool.wait_ge(ident_ready, 1)
            for n, (place, value) in enumerate(((mv[:, :, :], 1.0), (ssq[:, :], 1.0), (qT[96:128, :, :], 0.0),
                                                (k_diag[96:128, :, :, :], 0.0),
                                                (disp_diag[96:128, :, :, :], 0.0),
                                                (xn[96:128, :, :], 0.0))):
                pool.memset(place, value).then_inc(zeros_ready, 1)
                pool.wait_ge(zeros_ready, n + 1)

            def band(mask, pattern, width):
                step(pool.memset(mask, 1.0))
                step(pool.affine_select(out=mask, in_=mask, compare_op=ALU.is_ge, fill=0.0, base=0,
                                        pattern=[[-w, n] for w, n in pattern], channel_multiplier=1))
                step(pool.affine_select(out=mask, in_=mask, compare_op=ALU.is_ge, fill=0.0, base=width - 1,
                                        pattern=pattern, channel_multiplier=-1))

            band(head_mask[:, :], [[DH, HG]], DH)
            band(image_mask[:, :], [[N, TPI]], N)
            band(value_mask[:, :, :].rearrange("p g (j d) -> p g j d", j=3), [[0, G3], [N, 3], [0, DH]], N)
            v_blocks = v_diag[:, :, :, :].rearrange("p a b (g w) -> p (a b g) w", w=VW)
            pool.tensor_copy(v_blocks[0:TR, :, 3 * DH:VW],
                             image_mask[0:TR, :].unsqueeze(1).to_broadcast([TR, 16, 3])).then_inc(masks_ready, 1)

            for n in range(2):
                a, b = 3 * n, 3 * n + 3
                pool.wait_ge(moments, b)
                if n == 0:
                    pool.wait_ge(masks_ready, 1)
                step(pool.tensor_scalar(var_eps[:, a:b], mv[:, a:b, 1], EPS, None, ALU.add))
                pool.tensor_tensor(rstd[:, a:b], var_eps[:, a:b], neg_half[:, a:b], ALU.pow).then_inc(rstd_ready, 1)
            pool.wait_ge(slots_sq, 1)
            step(pool.tensor_scalar(slot_sc[0:S, 2:3], slot_sc[0:S, 0:1], EPS * EPS, None, ALU.max))
            step(pool.tensor_tensor(slot_sc[0:S, 3:4], slot_sc[0:S, 2:3], neg_half[0:S, 0:1], ALU.pow))
            pool.wait_ge(slots_in, 32)
            pool.tensor_tensor(slot_sc[0:S, 2:3], slot_sc[0:S, 3:4], slot_sc[0:S, 1:2],
                               ALU.mult).then_inc(slots_scaled, 1)

            def k_blocks(i):
                for og in range(OG):
                    pool.tensor_tensor(
                        k_diag[0:C2, i % 2, og, :].rearrange("p (a h m) -> p a h m", a=2, h=HG),
                        kT[0:C2, og, 2 * N * i:2 * N * (i + 1)].rearrange("p (a m) -> p a m", a=2)
                        .unsqueeze(2).to_broadcast([C2, 2, HG, N]),
                        head_mask[0:C2, :].unsqueeze(1).unsqueeze(3).to_broadcast([C2, 2, HG, N]),
                        ALU.mult).then_inc(kdiag_ready, 1)

            def ln_bias(i):
                if i == 0:
                    pool.wait_ge(ab_in, 16)
                pool.wait_ge(xn_ready, i + 1)
                pool.tensor_tensor(h[0:rows(i), i, :], h[0:rows(i), i, :], attn_b_row[0:rows(i), :],
                                   ALU.add).then_inc(bias_added, 1)

            def norm_floor(n):
                a, b = 2 * n, 2 * n + 2
                pool.wait_ge(moments2, b)
                step(pool.tensor_scalar(var_eps[:, a:b], mv[:, a:b, 1], 1.0 + EPS, EPS * EPS, ALU.mult, ALU.add))
                pool.tensor_scalar(floor[:, a:b], var_eps[:, a:b], EPS * EPS, None, ALU.mult).then_inc(floor_ready, 1)

            def rms_scale(n):
                a, b = 2 * n, 2 * n + 2
                pool.tensor_tensor(ln_scale[:, a:b], var_eps[:, a:b], neg_half[:, a:b],
                                   ALU.pow).then_inc(scale2_ready, 1)

            def rms_norms(n):
                a, b = 2 * n, 2 * n + 2
                pool.wait_ge(floored, n + 1)
                pool.tensor_tensor(rnorm[:, a:b], ssq[:, a:b], neg_half[:, a:b],
                                   ALU.pow).then_inc(rnorm_ready, 1)

            for i in range(PAIRS):
                pool.wait_ge(k_ready, 2 if i < 4 else 4)
                if i >= 2:
                    pool.wait_ge(scores_ready, i - 1)
                k_blocks(i)
                if i < TT:
                    ln_bias(i)

            norm_floor(0)
            rms_norms(0)
            rms_scale(0)
            pool.wait_ge(scores_ready, PAIRS)
            pool.memset(y_diag[:, :, :, :], 0.0).then_inc(ydiag_zero, 1)
            pool.wait_ge(ydiag_zero, 1)
            norm_floor(1)
            rms_norms(1)
            rms_scale(1)
            norm_floor(2)
            rms_norms(2)
            rms_scale(2)

            def select(g, gg):
                pool.tensor_copy(sel[0:S, gg, :].rearrange("p (s b) -> p s b", s=GS),
                                 ident[0:S, bass.ds(g * GS, GS)].unsqueeze(2).to_broadcast([S, GS, B])
                                 ).then_inc(sel_ready, 1)

            select(0, 0)
            select(1, 1)
            pool.wait_ge(y_done, TT)
            pool.memset(gact[:, :, :, :], 0.0).then_inc(gact_zero, 1)

            pool.wait_ge(y_kept_d, 2)
            pool.wait_ge(y_kept_a, 10)
            with pool.Fori(1, GROUPS // 2) as it:
                for gg in range(2):
                    g = it * 2 + gg
                    pool.wait_ge(units_used, g * UNITS + (3 - 2 * UNITS))
                    pool.tensor_copy(y_group[:, gg, :, :].rearrange("p j (q n) -> p j q n", q=4),
                                     y_diag[:, :, bass.ds(g * 4, 4), :]).then_inc(group_in, 1)
                    pool.wait_ge(mix_done, g - 1)
                    select(g, gg)

        @block.scalar
        def _(act):
            for n in range(0, 2 * GRID, 2):
                if n % GRID == 0:
                    act.wait_ge(x_in[n // 6], 16)
                    act.copy(*pixels(n // 6, 4, 6)).then_inc(regrouped_a, 1)
                act.wait_ge(x_turned, n + 1)
                ph, nw = n // 6, n % 6
                act.copy(patchesT[:, ph * 3:ph * 3 + 3, nw::GRID],
                         ps[:, n % 4, 0:288].rearrange("p (r n) -> p r n", r=3)).then_inc(x_kept_a, 1)
            for t in range(8):
                act.wait_ge(w_turned, t + 1)
                dst = qkvT[0:C2, :, t * C2:(t + 1) * C2] if t < 6 else projT[0:C2, :, (t - 6) * C2:(t - 5) * C2]
                act.copy(dst, ps[0:C2, t % 4, 0:2 * C2].rearrange("p (c n) -> p c n", c=2)).then_inc(w_kept, 1)
            act.wait_ge(slots_in, 32)
            act.activation(slot_squares[0:S, :], slot_rows[0:S, :], ACT.Square,
                           accum_out=slot_sc[0:S, 0:1]).then_inc(slots_sq, 1)

            def keep_xT(t):
                act.wait_ge(xn_turned, t + 1)
                act.copy(xT[0:C2, :, t * TR:t * TR + rows(t)],
                         ps[0:C2, t % 3, 0:2 * rows(t)].rearrange("p (c n) -> p c n", c=2)).then_inc(xT_ready, 1)

            def keep_q(half):
                for g in range(2):
                    act.wait_ge(qk_done, half * 4 + g + 1)
                    act.mul(qT[0:C2, g, half * HALF:(half + 1) * HALF],
                            ps[0:C2, 2 + g, 0:HALF], SCALE).then_inc(q_ready, 1)

            def copy_tokens(i):
                if i >= 2:
                    act.wait_ge(v_done, i - 1)
                for c in range(2):
                    act.copy(x_copies[0:C2, i % 2, c, :, :].rearrange("p a (j n) -> p a j n", j=3),
                             xT[0:C2, c, 2 * N * i:2 * N * (i + 1)].rearrange("p (a n) -> p a n", a=2)
                             .unsqueeze(2).to_broadcast([C2, 2, 3, N])).then_inc(copies_ready, 1)

            for t in range(3):
                keep_xT(t)
            act.wait_ge(misc_turned, 1)
            act.copy(b1T[:, :, :], ps[:, 6, 0:FC * S].rearrange("p (c s) -> p c s", c=FC)).then_inc(misc_kept, 1)
            keep_q(0)
            for t in range(3, TT):
                keep_xT(t)
            for t in range(3):
                act.wait_ge(xT_ready, t + 1)
            copy_tokens(0)
            keep_q(1)
            act.wait_ge(misc_turned, 2)
            act.copy(slotT[0:C2, :, :], ps[0:C2, 0, 256:256 + 2 * S].rearrange("p (c s) -> p c s", c=2)
                     ).then_inc(misc_kept, 1)

            def square(t):
                if t:
                    act.wait_ge(sq_ready, t)
                act.wait_ge(centered, t + 1)
                act.activation(squares[0:rows(t), :], xn[0:rows(t), t, :], ACT.Square,
                               accum_out=ssq[0:rows(t), t:t + 1]).then_inc(sq_ready, 1)

            def unit_tokens(part):
                act.wait_ge(rnorm_ready, part + 1)
                if part == 0:
                    act.wait_ge(v_done, PAIRS)
                for t in (2 * part, 2 * part + 1):
                    act.wait_ge(centered, t + 1)
                    act.mul(tok[0:rows(t), t, :], xn[0:rows(t), t, :], rnorm[0:rows(t), t:t + 1]).then_inc(tok_ready, 1)

            def keep_tokT(part):
                a, b = span(part)
                act.wait_ge(tok_turned, part + 1)
                act.copy(xT[0:C2, :, a:b],
                         ps[0:C2, 2 + part % 2, 0:2 * (b - a)].rearrange("p (c n) -> p c n", c=2)).then_inc(tokT_ready, 1)

            def keep_oT(p):
                act.wait_ge(o_turned, p + 1)
                src = ps[0:C2, 6 + p % 2, 256:256 + 2 * R2].rearrange("p (c n) -> p c n", c=2)
                for a in range(2):
                    act.copy(oT[0:C2, :, (2 * p + a) * N:(2 * p + a + 1) * N],
                             src[:, :, 64 * a:64 * a + N]).then_inc(oT_ready, 1)

            def keep_probsT(p):
                act.wait_ge(probs_turned, p + 1)
                if p >= 2:
                    act.wait_ge(pv_done, p - 1)
                act.copy(probsT[0:TR, p % 2, :, :],
                         ps[0:TR, p % 2, 0:G3 * R2].rearrange("p (g n) -> p g n", g=G3)).then_inc(probsT_ready, 1)

            def keep_logits(part):
                act.wait_ge(logits_done, part + 1)
                a, b = span(part)
                act.copy(logits[0:S, a:b], ps[0:S, part % 2, 0:b - a]).then_inc(logits_ready, 1)

            def exp_dispatch(part):
                act.wait_ge(d_shifted, part + 1)
                a, b = span(part)
                act.activation(disp[0:S, a:b], disp[0:S, a:b], ACT.Exp).then_inc(d_exp, 1)

            def keep_y(row, t):
                n, col = min(TPI, B - TPI * t), TPI * t + (B if row else 0)
                act.wait_ge(y_done, t + 1)
                if t == 0:
                    act.wait_ge(ydiag_zero, 1)
                act.copy(y_diag[row:row + 64, :, :, col:col + n], y_columns(row, t, n)).then_inc(y_kept_a, 1)

            act.wait_ge(xT_ready, TT)
            for i in range(PAIRS):
                if i >= 1:
                    keep_probsT(i - 1)
                act.wait_ge(shifted, i + 1)
                act.activation(probs[0:R2, i % 2, :], probs[0:R2, i % 2, :], ACT.Exp).then_inc(exp_ready, 1)
                if i + 1 < PAIRS:
                    copy_tokens(i + 1)
                if i >= 2:
                    keep_oT(i - 2)
                if i == 6:
                    square(0)
                    square(1)
            keep_probsT(PAIRS - 1)
            unit_tokens(0)
            square(2)
            keep_oT(PAIRS - 2)
            keep_tokT(0)
            keep_oT(PAIRS - 1)
            square(3)
            square(4)
            unit_tokens(1)
            square(5)
            keep_tokT(1)
            exp_dispatch(0)
            unit_tokens(2)
            keep_logits(0)
            keep_tokT(2)
            exp_dispatch(1)
            keep_logits(1)
            exp_dispatch(2)
            for t in (0, 1):
                for row in (0, 64):
                    keep_y(row, t)
            keep_logits(2)
            for t in (2, 3):
                for row in (0, 64):
                    keep_y(row, t)
            for t in (4, 5):
                keep_y(64, t)

            def mlp_group(g, gg, it):
                static = isinstance(g, int)
                if static and g == 0:
                    act.wait_ge(c_shifted, 1)
                    act.activation(comb[0:TR, :, :], comb[0:TR, :, :], ACT.Exp).then_inc(c_exp, 1)
                act.wait_ge(units_used, g * UNITS + 3)
                earlier(act, hid_turned, g)
                for half in range(2):
                    act.copy(hid[:, :, half * 64:(half + 1) * 64].rearrange("p c n -> p n c"),
                             ps[:, half, 0:FF // 2].rearrange("p (n c) -> p n c", c=FC)).then_inc(hid_ready, 1)
                if static and g == 0:
                    act.wait_ge(comb_turned, 1)
                    act.copy(combT[0:S, 0:4 * TR], ps[0:S, 7, 0:4 * TR]).then_inc(combT_ready, 1)
                    act.wait_ge(comb_turned, 2)
                    act.copy(combT[0:S, 4 * TR:NT], ps[0:S, 4, 0:NT - 4 * TR]).then_inc(combT_ready, 1)
                    act.wait_ge(gact_zero, 1)
                act.wait_ge(pre_ready, g * 2 + 2)
                earlier(act, units_used, g * UNITS)
                gflat = gact[:, :, :, :].rearrange("p c s n -> p (c s n)").rearrange("p (k n) -> p k n", n=64)
                src = pre[:, :, :].rearrange("p c (q l b) -> p (c q) l b", l=2, b=B)
                for l in range(2):
                    act.activation(gflat[:, :, 48 * l:48 * l + B], src[:, :, l, :], ACT.Gelu).then_inc(gact_ready, 1)
                act.wait_ge(units_used, g * UNITS + 6)
                act.copy(y2[:, gg, :], ps[:, 4, 0:D]).then_inc(y2_ready, 1)

            for gg in range(2):
                mlp_group(gg, gg, 0)
            with act.Fori(1, GROUPS // 2) as it:
                for gg in range(2):
                    mlp_group(it * 2 + gg, gg, it)

        @block.vector
        def _(dve):
            steps = [0]

            def step(ins):
                steps[0] += 1
                ins.then_inc(dve_step, 1)
                dve.wait_ge(dve_step, steps[0])

            for n in range(1, 2 * GRID, 2):
                if n % 6 == 1:
                    for a in (0, 2):
                        dve.wait_ge(x_in[n // 6], 16)
                        dve.tensor_copy(*pixels(n // 6, a, a + 2)).then_inc(regrouped_d, 1)
                dve.wait_ge(x_turned, n + 1)
                ph, nw = n // 6, n % 6
                dve.tensor_copy(patchesT[:, ph * 3:ph * 3 + 3, nw::GRID],
                                ps[:, n % 4, 0:288].rearrange("p (r n) -> p r n", r=3)).then_inc(x_kept_d, 1)

            def embed_tile(t):
                dve.wait_ge(embedded, t + 1)
                r = rows(t)
                step(dve.tensor_tensor(h[0:r, t, :], ps[0:r, 4 + t % 4, 0:D], pos_b[0:r, :], ALU.add))
                dve.bn_stats(stats[0:r, t, :], h[0:r, t, :]).then_inc(h_ready, 1)
                dve.wait_ge(h_ready, t + 1)
                dve.bn_aggr(mv[0:r, t, :], stats[0:r, t, :]).then_inc(moments, 1)

            def norm_tile(t):
                r = rows(t)
                dve.wait_ge(rstd_ready, 1 + t // 3)
                dve.wait_ge(moments, t + 1)
                dve.tensor_scalar(xn[0:r, t, :], h[0:r, t, :], mv[0:r, t, 0:1], rstd[0:r, t:t + 1],
                                  ALU.subtract, ALU.mult).then_inc(xn_ready, 1)

            dve.wait_ge(pos_in, 64)
            step(dve.tensor_tensor(pos_b[0:TR, :], pos_b[0:TR, :], pos_raw[0:TR, :], ALU.add))
            dve.wait_ge(zeros_ready, 6)
            for t in range(4):
                embed_tile(t)
            for t in range(3):
                norm_tile(t)
            for t in range(4, TT):
                embed_tile(t)
            for t in range(3, TT):
                norm_tile(t)
            step(dve.tensor_reduce(batch_mask[:, :], ident[:, :].rearrange("p (s b) -> p b s", b=B), AX.X, ALU.add))
            dve.wait_ge(slots_scaled, 1)
            dve.tensor_scalar(slot_rows[0:S, :], slot_rows[0:S, :], slot_sc[0:S, 2:3], None,
                              ALU.mult).then_inc(slots_ready, 1)
            for bank in (4, 5):
                dve.memset(ps[32:64, bank, 0:OG * QW], 0.0).then_inc(junk_set, 1)

            def keep_k(half):
                for g in range(2):
                    dve.wait_ge(qk_done, half * 4 + g + 3)
                    dve.tensor_copy(kT[0:C2, g, half * HALF:(half + 1) * HALF],
                                    ps[0:C2, 2 + g, 0:HALF]).then_inc(k_ready, 1)

            keep_k(0)
            dve.wait_ge(misc_kept, 1)
            for bank in (6, 7):
                dve.memset(ps[32:64, bank, 0:G3 * VW], 1.0).then_inc(junk_set, 1)
            keep_k(1)
            dve.wait_ge(masks_ready, 1)

            def attn_tile(t, bank):
                r = rows(t)
                dve.wait_ge(attn_done, t + 1)
                dve.wait_ge(bias_added, t + 1)
                dve.tensor_tensor(h[0:r, t, :], ps[0:r, bank, 0:D], h[0:r, t, :], ALU.add).then_inc(h2_ready, 1)
                dve.wait_ge(h2_ready, t + 1)
                step(dve.bn_stats(stats[0:r, t, :], h[0:r, t, :]))
                dve.bn_aggr(mv[0:r, t, :], stats[0:r, t, :]).then_inc(moments2, 1)

            def center(t):
                r = rows(t)
                if t == 0:
                    dve.wait_ge(nw_in, 16)
                dve.wait_ge(moments2, t + 1)
                dve.scalar_tensor_tensor(out=xn[0:r, t, :], in0=h[0:r, t, :], scalar=mv[0:r, t, 0:1],
                                         in1=norm_row[0:r, :], op0=ALU.subtract, op1=ALU.mult).then_inc(centered, 1)

            def floor_norms(n):
                dve.wait_ge(floor_ready, n + 1)
                dve.wait_ge(sq_ready, 2 * n + 2)
                a, b = 2 * n, 2 * n + 2
                dve.tensor_tensor(ssq[:, a:b], ssq[:, a:b], floor[:, a:b], ALU.max).then_inc(floored, 1)

            def finish_pair(p):
                o_ps = ps[0:R2, 6 + p % 2, 0:G3 * VW].rearrange("p (g w) -> p g w", w=VW)
                dve.wait_ge(pv_done, p + 1)
                step(dve.reciprocal(rcp[0:R2, p % 2, :].rearrange("p (g j) -> p g j", g=G3),
                                    o_ps[:, :, 3 * DH:VW]))
                if p >= 2:
                    dve.wait_ge(o_turned, p - 1)
                dve.tensor_tensor(
                    o_rows[0:R2, p % 2, :].rearrange("p (g j d) -> p g j d", g=G3, j=3),
                    o_ps[:, :, 0:3 * DH].rearrange("p g (j d) -> p g j d", j=3),
                    rcp[0:R2, p % 2, :].rearrange("p (g j) -> p g j", g=G3).unsqueeze(3)
                    .to_broadcast([R2, G3, 3, DH]), ALU.mult).then_inc(o_ready, 1)

            def shift_dispatch(part):
                a, b = span(part)
                lg = ps[0:S, part % 2, 0:b - a].rearrange("p (b n) -> p b n", n=N)
                dg = disp[0:S, a:b].rearrange("p (b n) -> p b n", n=N)
                a, b = a // N, b // N
                dve.wait_ge(logits_done, part + 1)
                step(dve.tensor_reduce(soft[0:S, 0, a:b], lg, AX.X, ALU.max))
                dve.tensor_tensor(dg, lg, soft[0:S, 0, a:b].unsqueeze(2).to_broadcast([S, b - a, N]),
                                  ALU.subtract).then_inc(d_shifted, 1)

            def normalise_dispatch(first, last):
                a, b = span(first)[0], span(last)[1]
                dg = disp[0:S, a:b].rearrange("p (b n) -> p b n", n=N)
                a, b = a // N, b // N
                dve.wait_ge(d_exp, last + 1)
                step(dve.tensor_reduce(soft[0:S, 2, a:b], dg, AX.X, ALU.add))
                step(dve.reciprocal(soft[0:S, 3, a:b], soft[0:S, 2, a:b]))
                dve.tensor_tensor(dg, dg, soft[0:S, 3, a:b].unsqueeze(2).to_broadcast([S, b - a, N]),
                                  ALU.mult).then_inc(disp_ready, 1)

            def diag_dispatch(part):
                dve.wait_ge(disp_turned, part + 1)
                dve.wait_ge(scale2_ready, part + 1)
                for n, t in enumerate((2 * part, 2 * part + 1)):
                    r, m = rows(t), min(TPI, B - TPI * t)
                    dve.scalar_tensor_tensor(
                        out=disp_diag[0:r, t, 0:m, :],
                        in0=ps[0:r, 6 + part % 2, n * S:(n + 1) * S].unsqueeze(1).to_broadcast([r, m, S]),
                        scalar=ln_scale[0:r, t:t + 1],
                        in1=image_mask[0:r, 0:m].unsqueeze(2).to_broadcast([r, m, S]),
                        op0=ALU.mult, op1=ALU.mult).then_inc(ddiag_ready, 1)

            for i in range(PAIRS):
                sc = ps[0:R2, 4 + i % 2, 0:OG * QW].rearrange("p (h m) -> p h m", m=N)
                dve.wait_ge(scores_ready, i + 1)
                step(dve.tensor_reduce(mx[0:R2, i % 2, :], sc, AX.X, ALU.max))
                if i >= 2:
                    dve.wait_ge(probs_turned, i - 1)
                dve.tensor_tensor(probs[0:R2, i % 2, :].rearrange("p (h m) -> p h m", m=N), sc,
                                  mx[0:R2, i % 2, :].unsqueeze(2).to_broadcast([R2, HEADS, N]),
                                  ALU.subtract).then_inc(shifted, 1)
                for t, bank in attn_tiles(i):
                    attn_tile(t, bank)
                dve.wait_ge(v_done, i + 1)
                if i >= 2:
                    dve.wait_ge(pv_done, i - 1)
                dve.tensor_tensor(
                    v_diag[0:TR, i % 2, :, :].rearrange("p a (g w) -> p a g w", w=VW)[:, :, :, 0:3 * DH],
                    ps[0:TR, 2 + i % 2, 0:2 * D].rearrange("p (a g w) -> p a g w", a=2, g=G3),
                    value_mask[0:TR, :, :].unsqueeze(1).to_broadcast([TR, 2, G3, 3 * DH]),
                    ALU.mult).then_inc(vdiag_ready, 1)
                if i >= 1:
                    finish_pair(i - 1)
                for t, bank in attn_tiles(i):
                    center(t)
                if i == 6:
                    floor_norms(0)
            finish_pair(PAIRS - 1)
            attn_tile(3, attn_tiles(PAIRS)[0][1])
            center(3)
            for t, bank in attn_tiles(PAIRS + 2):
                attn_tile(t, bank)
                center(t)
                if t == 4:
                    floor_norms(1)
            floor_norms(2)
            shift_dispatch(0)
            normalise_dispatch(0, 0)
            shift_dispatch(1)
            diag_dispatch(0)
            shift_dispatch(2)
            normalise_dispatch(1, 2)
            diag_dispatch(1)
            dve.memset(ps[:, 7, (TT - 1) * S:TT * S], 0.0).then_inc(soft_bank, 1)
            diag_dispatch(2)

            def keep_mix(g, gg):
                dve.wait_ge(mix_done, g + 1)
                dve.tensor_tensor(mix[:, gg, :].rearrange("p (h b n) -> p h b n", h=2, n=N),
                                  ps[:, 0:2, 0:HALF].rearrange("p h (b n) -> p h b n", n=N),
                                  batch_mask[:, :].rearrange("p (h b) -> p h b", h=2).unsqueeze(3)
                                  .to_broadcast([128, 2, B // 2, N]), ALU.mult).then_inc(mix_ready, 1)

            for t in (4, 5):
                n = min(TPI, B - TPI * t)
                dve.wait_ge(y_done, t + 1)
                dve.wait_ge(ydiag_zero, 1)
                dve.tensor_copy(y_diag[0:64, :, :, TPI * t:TPI * t + n],
                                y_columns(0, t, n)).then_inc(y_kept_d, 1)
            ct = ps[0:TR, 7, 0:TT * S].rearrange("p (t s) -> p t s", t=TT)
            dve.wait_ge(logits_turned, 1)
            step(dve.tensor_reduce(soft[0:TR, 1, 0:TT], ct, AX.X, ALU.max))
            dve.wait_ge(tok_turned, PARTS)
            dve.tensor_tensor(comb[0:TR, :, :], ct, soft[0:TR, 1, 0:TT].unsqueeze(2).to_broadcast([TR, TT, S]),
                              ALU.subtract).then_inc(c_shifted, 1)
            dve.wait_ge(c_exp, 1)
            step(dve.tensor_reduce(soft[0:TR, 1, 8:8 + TT], comb[0:TR, :, :], AX.X, ALU.add))
            step(dve.reciprocal(soft[0:TR, 1, 0:TT], soft[0:TR, 1, 8:8 + TT]))
            dve.tensor_tensor(comb[0:TR, :, :], comb[0:TR, :, :],
                              soft[0:TR, 1, 0:TT].unsqueeze(2).to_broadcast([TR, TT, S]),
                              ALU.mult).then_inc(comb_ready, 1)

            def mlp_group(g, gg, it):
                dve.wait_ge(hid_turned, g + 1)
                earlier(dve, gact_ready, g * 2)
                for half in range(2):
                    dve.tensor_tensor(
                        pre[:, 3 * half:3 * half + 3, :].rearrange("p c (s b) -> p c s b", s=GS),
                        ps[:, 2 + half, 0:384].rearrange("p (c s b) -> p c s b", c=3, s=GS),
                        b1T[:, 3 * half:3 * half + 3, bass.ds(g * GS, GS)].unsqueeze(3)
                        .to_broadcast([128, 3, GS, B]), ALU.add).then_inc(pre_ready, 1)
                keep_mix(g, gg)

            for gg in range(2):
                mlp_group(gg, gg, 0)
            with dve.Fori(1, GROUPS // 2) as it:
                for gg in range(2):
                    mlp_group(it * 2 + gg, gg, it)

            for tt in range(2):
                dve.wait_ge(combined, (GROUPS - 1) * 3 + tt + 1)
                dve.tensor_tensor(h[0:TR, 2 * tt:2 * tt + 2, :],
                                  ps[0:TR, 5 + tt, 0:2 * D].rearrange("p (t d) -> p t d", t=2),
                                  h[0:TR, 2 * tt:2 * tt + 2, :], ALU.add).then_inc(final_ready, 1)
            dve.wait_ge(combined, GROUPS * 3)
            for t in (TT - 2, TT - 1):
                dve.tensor_tensor(h[0:rows(t), t, :], ps[0:rows(t), 7, (t % 2) * D:(t % 2 + 1) * D],
                                  h[0:rows(t), t, :], ALU.add).then_inc(final_ready, 1)

        @block.tensor
        def _(pe):
            def keep_busy(bank, count):
                for _ in range(count):
                    pe.matmul(ps[:, bank, 0:128], ident[:, :], ident[:, :], start=True, stop=True)

            def embed(t, chunks=range(KC)):
                if t >= 4:
                    pe.wait_ge(h_ready, t - 3)
                for c in chunks:
                    mm = pe.matmul(ps[0:rows(t), 4 + t % 4, 0:D], patchesT[:, c, t * TR:t * TR + rows(t)],
                                   embed_w[:, c, :], start=(c == 0), stop=(c == KC - 1))
                if chunks[-1] == KC - 1:
                    mm.then_inc(embedded, 1)

            pe.wait_ge(ident_ready, 1)
            keep_busy(7, 9)
            for n in range(2 * GRID):
                if n == 6:
                    keep_busy(7, 2)
                    pe.wait_ge(wp_in, 16)
                    pe.wait_ge(x_kept_a, 3)
                    pe.wait_ge(x_kept_d, 3)
                    for t in range(2):
                        embed(t, range(3))
                ph, nw = n // 6, n % 6
                if nw < 4:
                    pe.wait_ge(regrouped_d, 2 * ph + nw // 2 + 1)
                else:
                    pe.wait_ge(regrouped_a, ph + 1)
                if n >= 4:
                    pe.wait_ge(x_kept_d if n % 2 else x_kept_a, (n - 4) // 2 + 1)
                for r in range(3):
                    mm = pe.transpose(ps[:, n % 4, r * C2:(r + 1) * C2],
                                      x_patch[0:C2, ph, nw, r * 128:(r + 1) * 128], ident[0:C2, 0:C2])
                mm.then_inc(x_turned, 1)
            embed(2, range(3))
            embed(3, range(3))
            pe.wait_ge(x_kept_a, 6)
            pe.wait_ge(x_kept_d, 6)

            def turn_weights(a, b):
                for t in range(a, b):
                    pe.wait_ge(wqkv_in if t < 6 else wproj_in, 16)
                    if t >= 4:
                        pe.wait_ge(w_kept, t - 3)
                    for c in range(2):
                        cols = slice(c * C2, (c + 1) * C2)
                        raw = qkv_raw[0:C2, t, cols] if t < 6 else proj_raw[0:C2, t - 6, cols]
                        mm = pe.transpose(ps[0:C2, t % 4, cols], raw, ident[0:C2, 0:C2])
                    mm.then_inc(w_turned, 1)

            def turn_xn(t):
                pe.wait_ge(xn_ready, t + 1)
                if t >= 3:
                    pe.wait_ge(xT_ready, t - 2)
                if t == 5:
                    pe.wait_ge(k_ready, 1)
                r = rows(t)
                for c in range(2):
                    mm = pe.transpose(ps[0:C2, t % 3, c * r:(c + 1) * r], xn[0:r, t, c * C2:(c + 1) * C2],
                                      ident[0:r, 0:r])
                mm.then_inc(xn_turned, 1)

            def project_qk(half, groups):
                pe.wait_ge(xT_ready, 3 if half == 0 else TT)
                for g in groups:
                    if half or g >= 2:
                        n = half * 4 + g - 2
                        pe.wait_ge(q_ready if n % 4 < 2 else k_ready, n // 4 * 2 + n % 2 + 1)
                    for c in range(2):
                        mm = pe.matmul(ps[0:C2, 2 + g % 2, 0:HALF], qkvT[0:C2, c, g * C2:(g + 1) * C2],
                                       xT[0:C2, c, half * HALF:(half + 1) * HALF], start=(c == 0), stop=(c == 1))
                    mm.then_inc(qk_done, 1)

            def scores(i):
                pe.wait_ge(kdiag_ready, 2 * (i + 1))
                if i == 0:
                    pe.wait_ge(junk_set, 4)
                    pe.wait_ge(q_ready, 2)
                elif i == 1:
                    pe.wait_ge(q_ready, 4)
                else:
                    pe.wait_ge(shifted, i - 1)
                for og in range(OG):
                    for a in range(2):
                        mm = pe.matmul(ps[64 * a:64 * a + N, 4 + i % 2, og * QW:(og + 1) * QW],
                                       qT[:, og, (2 * i + a) * N:(2 * i + a + 1) * N],
                                       k_diag[:, i % 2, og, a * QW:(a + 1) * QW], start=True, stop=True)
                mm.then_inc(scores_ready, 1)

            def turn_probs(p):
                pe.wait_ge(exp_ready, p + 1)
                if p == 0:
                    pe.wait_ge(misc_kept, 2)
                if p >= 2:
                    pe.wait_ge(probsT_ready, p - 1)
                for g in range(G3):
                    mm = pe.transpose(ps[0:TR, p % 2, g * R2:(g + 1) * R2],
                                      probs[0:R2, p % 2, g * TR:(g + 1) * TR], ident[0:R2, 0:R2])
                mm.then_inc(probs_turned, 1)

            def values(i):
                pe.wait_ge(copies_ready, 2 * (i + 1))
                if i < 2:
                    pe.wait_ge(k_ready, 3 + i)
                else:
                    pe.wait_ge(vdiag_ready, i - 1)
                for a in range(2):
                    for c in range(2):
                        mm = pe.matmul(ps[0:TR, 2 + i % 2, a * D:(a + 1) * D], x_copies[0:C2, i % 2, c, a, :],
                                       qkvT[0:C2, c, 2 * D:3 * D], start=(c == 0), stop=(c == 1))
                mm.then_inc(v_done, 1)

            def probs_times_values(p):
                pe.wait_ge(probsT_ready, p + 1)
                pe.wait_ge(vdiag_ready, p + 1)
                if p >= 2:
                    pe.wait_ge(oT_ready, 2 * (p - 1))
                done = sum(len(attn_tiles(n)) for n in range(min(p + 1, PAIRS - 1) + 1))
                if done:
                    pe.wait_ge(h2_ready, min(done, 3))
                for g in range(G3):
                    for a in range(2):
                        mm = pe.matmul(ps[64 * a:64 * a + N, 6 + p % 2, g * VW:(g + 1) * VW],
                                       probsT[0:TR, p % 2, g, 64 * a:64 * a + N],
                                       v_diag[0:TR, p % 2, a, g * VW:(g + 1) * VW], start=True, stop=True)
                mm.then_inc(pv_done, 1)

            def turn_output(p):
                pe.wait_ge(o_ready, p + 1)
                for c in range(2):
                    mm = pe.transpose(ps[0:C2, 6 + p % 2, 256 + c * R2:256 + (c + 1) * R2],
                                      o_rows[0:R2, p % 2, c * C2:(c + 1) * C2], ident[0:R2, 0:R2])
                mm.then_inc(o_turned, 1)

            def project_output(t, bank, i):
                r = rows(t)
                pe.wait_ge(oT_ready, 2 * (i - 2))
                if i >= PAIRS:
                    pe.wait_ge(shifted, PAIRS)
                    pe.wait_ge(h2_ready, 3 if t < 5 else 4)
                for c in range(2):
                    mm = pe.matmul(ps[0:r, bank, 0:D], oT[0:C2, c, t * TR:t * TR + r], projT[0:C2, c, :],
                                   start=(c == 0), stop=(c == 1))
                mm.then_inc(attn_done, 1)

            def turn_tok(part):
                a, b = span(part)
                pe.wait_ge(tok_ready, 2 * part + 2)
                pe.wait_ge(vdiag_ready, PAIRS)
                if part == 2:
                    pe.wait_ge(tokT_ready, 1)
                for c in range(2):
                    for t in (2 * part, 2 * part + 1):
                        col = c * (b - a) + t * TR - a
                        mm = pe.transpose(ps[0:C2, 2 + part % 2, col:col + rows(t)],
                                          tok[0:rows(t), t, c * C2:(c + 1) * C2], ident[0:rows(t), 0:rows(t)])
                mm.then_inc(tok_turned, 1)

            def logit_sums(part):
                a, b = span(part)
                pe.wait_ge(tokT_ready, part + 1)
                pe.wait_ge(probsT_ready, PAIRS)
                if part == 2:
                    pe.wait_ge(logits_ready, 1)
                    pe.wait_ge(d_shifted, 1)
                for c in range(2):
                    mm = pe.matmul(ps[0:S, part % 2, 0:b - a], slotT[0:C2, c, :], xT[0:C2, c, a:b],
                                   start=(c == 0), stop=(c == 1))
                mm.then_inc(logits_done, 1)

            def turn_dispatch(part):
                pe.wait_ge(disp_ready, min(part + 1, 2))
                pe.wait_ge(oT_ready, 2 * PAIRS)
                if part == 2:
                    pe.wait_ge(ddiag_ready, 2)
                for n, t in enumerate((2 * part, 2 * part + 1)):
                    mm = pe.transpose(ps[0:rows(t), 6 + part % 2, n * S:(n + 1) * S],
                                      disp[0:S, t * TR:t * TR + rows(t)], ident[0:S, 0:S])
                mm.then_inc(disp_turned, 1)

            def slot_inputs(t):
                pe.wait_ge(ddiag_ready, t + 1)
                if t == 0:
                    pe.wait_ge(tokT_ready, 2)
                    pe.wait_ge(h2_ready, TT)
                elif t >= 3:
                    pe.wait_ge(y_kept_a, 2 * (t - 2))
                r, n = 128 if t < TT - 1 else rows(t), min(TPI, B - TPI * t)
                for j in range(3):
                    for l in range(2):
                        mm = pe.matmul(ps[64 * l:64 * l + 64, 3 + t % 3, j * 96:j * 96 + n * S // 2],
                                       xn[0:r, t, j::3],
                                       disp_diag[0:r, t, 0:n, :].rearrange("p b (q l) -> p b q l", l=2)[:, :, :, l],
                                       start=True, stop=True)
                mm.then_inc(y_done, 1)

            for t in range(3):
                embed(t, range(3, KC))
            turn_weights(0, 4)
            embed(3, range(3, KC))
            turn_weights(4, 8)
            embed(4)
            pe.wait_ge(w_kept, 8)
            for t in range(3):
                turn_xn(t)
            embed(5)
            pe.wait_ge(b1_in, 16)
            pe.wait_ge(h_ready, 3)
            b1v = b1_raw[0:S, :].rearrange("s (p c) -> s c p", c=FC)
            for c in range(FC):
                mm = pe.transpose(ps[:, 6, c * S:(c + 1) * S], b1v[:, c, :], ident[0:S, 0:S])
            mm.then_inc(misc_turned, 1)
            project_qk(0, range(4))
            for t in range(3, TT):
                turn_xn(t)
            project_qk(1, range(2))
            pe.wait_ge(slots_ready, 1)
            pe.wait_ge(xT_ready, TT)
            for c in range(2):
                mm = pe.transpose(ps[0:C2, 0, 256 + c * S:256 + (c + 1) * S], slot_rows[0:S, c * C2:(c + 1) * C2],
                                  ident[0:S, 0:S])
            mm.then_inc(misc_turned, 1)
            scores(0)
            project_qk(1, range(2, 4))

            for i in range(PAIRS):
                if i:
                    scores(i)
                    turn_probs(i - 1)
                for t, bank in attn_tiles(i):
                    project_output(t, bank, i)
                values(i)
                if i:
                    probs_times_values(i - 1)
                if i >= 2:
                    turn_output(i - 2)
            turn_probs(PAIRS - 1)
            for t, bank in attn_tiles(PAIRS):
                project_output(t, bank, PAIRS)
            probs_times_values(PAIRS - 1)
            turn_output(PAIRS - 2)
            turn_tok(0)
            turn_output(PAIRS - 1)
            for t, bank in attn_tiles(PAIRS + 2):
                project_output(t, bank, PAIRS + 2)
            logit_sums(0)
            keep_busy(7, 8)
            turn_tok(1)
            keep_busy(7, 2)
            logit_sums(1)
            turn_tok(2)
            turn_dispatch(0)
            logit_sums(2)
            slot_inputs(0)
            slot_inputs(1)
            keep_busy(2, 6)
            turn_dispatch(1)
            turn_dispatch(2)
            keep_busy(2, 2)
            slot_inputs(2)
            slot_inputs(3)
            slot_inputs(4)
            slot_inputs(5)
            pe.wait_ge(y_kept_d, 2)
            pe.wait_ge(y_kept_a, 10)
            pe.wait_ge(logits_ready, PARTS)

            def turn_logits():
                pe.wait_ge(soft_bank, 1)
                for t in range(TT):
                    mm = pe.transpose(ps[0:rows(t), 7, t * S:(t + 1) * S], logits[0:S, t * TR:t * TR + rows(t)],
                                      ident[0:S, 0:S])
                mm.then_inc(logits_turned, 1)

            def turn_combine():
                pe.wait_ge(comb_ready, 1)
                for t in range(TT):
                    bank, col = (7, t * TR) if t < 4 else (4, (t - 4) * TR)
                    mm = pe.transpose(ps[0:S, bank, col:col + rows(t)], comb[0:rows(t), t, :],
                                      ident[0:rows(t), 0:rows(t)])
                    if t in (3, TT - 1):
                        mm.then_inc(comb_turned, 1)

            def open_output(t):
                r = rows(t)
                pe.matmul(ps[0:r, 5 + t // 2, (t % 2) * D:(t % 2 + 1) * D], combT[0:S, t * TR:t * TR + r],
                          b2_rows[0:S, :], start=(t % 2 == 0), stop=False, skip_group_check=True)

            def mix_weights(g, gg):
                pe.wait_ge(sel_ready, g + 1)
                for half in range(2):
                    mm = pe.matmul(ps[:, half, 0:HALF], sel[0:S, gg, :],
                                   combT[0:S, half * HALF:(half + 1) * HALF], start=True, stop=True)
                mm.then_inc(mix_done, 1)

            def combine(g, gg):
                pe.wait_ge(y2_ready, g + 1)
                pe.wait_ge(mix_ready, g + 1)
                for t in range(TT):
                    r = rows(t)
                    mm = pe.matmul(ps[0:r, 5 + t // 2, (t % 2) * D:(t % 2 + 1) * D],
                                   mix[:, gg, t * TR:t * TR + r], y2[:, gg, :],
                                   start=False, stop=False, skip_group_check=True)
                    if t % 2:
                        mm.then_inc(combined, 1)

            def mlp_group(g, gg, it):
                static = isinstance(g, int)
                earlier(pe, mix_ready, g)
                if not static:
                    pe.wait_ge(group_in, g - 1)
                for j in range(3):
                    slot = gg * UNITS + j
                    pe.wait_ge(unit_in[slot], it * 16 + 16)
                    w = ring[:, slot, :].rearrange("p (q o) -> p q o", q=4)
                    for half in range(2):
                        for q in range(4):
                            y = y_diag[:, j, 4 * g + q, :] if static else y_group[:, gg, j, 32 * q:32 * q + 32]
                            mm = pe.matmul(ps[32 * q:32 * q + 32, half, 0:FF // 2], y,
                                           w[:, q, half * FF // 2:(half + 1) * FF // 2],
                                           start=(j == 0), stop=(j == 2), tile_position=(0, 32 * q))
                    mm.then_inc(units_used, 1)
                    if j == 0 and static and g == 0:
                        turn_logits()
                    elif j == 0:
                        combine(g - 1, 1 - gg)
                    elif j == 1 and not static:
                        keep_busy(3, 8)
                if static and g == 0:
                    turn_combine()
                pe.wait_ge(hid_ready, g * 2 + 2)
                earlier(pe, pre_ready, g * 2)
                for c in range(FC):
                    mm = pe.transpose(ps[:, 2 + c // 3, (c % 3) * 128:(c % 3 + 1) * 128], hid[:, c, :], ident[:, :])
                mm.then_inc(hid_turned, 1)
                if static and g == 0:
                    pe.wait_ge(combT_ready, 2)
                    pe.wait_ge(b2_in, 16)
                    for t in range(TT):
                        open_output(t)
                mix_weights(g, gg)
                if not static:
                    keep_busy(4, 4)
                pe.wait_ge(gact_ready, g * 2 + 2)
                earlier(pe, y2_ready, g)
                for u in range(3):
                    slot = gg * UNITS + 3 + u
                    if u == 2 and not static:
                        keep_busy(3, 9)
                    w = ring[:, slot, :].rearrange("p (s c d) -> p s c d", s=GS, c=2)
                    pe.wait_ge(unit_in[slot], it * 16 + 16)
                    for cc in range(2):
                        for l in range(2):
                            for q in range(4):
                                first = u == 0 and cc == 0 and l == 0
                                last = u == 2 and cc == 1 and l == 1
                                mm = pe.matmul(ps[32 * q:32 * q + 32, 4, 0:D], gact[:, 2 * u + cc, 2 * q + l, :],
                                               w[:, 2 * q + l, cc, :], start=first, stop=last,
                                               tile_position=(0, 32 * q))
                    mm.then_inc(units_used, 1)

            for gg in range(2):
                mlp_group(gg, gg, 0)
            with pe.Fori(1, GROUPS // 2) as it:
                for gg in range(2):
                    mlp_group(it * 2 + gg, gg, it)
            combine(GROUPS - 1, 1)


_INS = ['x', 'L0_tok_W_proj', 'L0_tok_b_proj', 'L0_tok_pos_emb', 'L0_attn_w_qkv', 'L0_attn_w_proj',
        'L0_attn_b_proj', 'L0_ffn_slots', 'L0_ffn_scale', 'L0_ffn_fc1_weight', 'L0_ffn_fc1_bias',
        'L0_ffn_fc2_weight', 'L0_ffn_fc2_bias', 'L0_ffn_norm_weight']
_OUTS = [((16, 36, 192), 'float32')]


def kernel(**inputs):
    import numpy as _np
    import concourse.bacc as _bacc
    from concourse import mybir as _mybir
    from concourse.bass_utils import run_bass_kernel_spmd as _run

    nc = _bacc.Bacc("TRN2", target_bir_lowering=False, num_devices=1)
    arrays, args = {}, []
    for name in _INS:
        a = _np.ascontiguousarray(inputs[name])
        arrays[f"in_{name}_dram"] = a
        args.append(nc.dram_tensor(f"in_{name}_dram", a.shape, _mybir.dt.from_np(a.dtype), kind="ExternalInput").ap())
    for i, (shape, dtype) in enumerate(_OUTS):
        dt = _mybir.dt.from_np(_np.dtype(dtype))
        args.append(nc.dram_tensor(f"out_{i}_dram", shape, dt, kind="ExternalOutput").ap())
    vit_tower_kernel(nc, *args)
    r = _run(nc, [arrays], core_ids=[0])
    return r.results[0]["out_0_dram"]
```
